# Optimizing a Trainium2 kernel written in Bass

```python
import numpy as np
import jax
import jax.numpy as jnp

def _softmax(x, axis=-1):
    return jax.nn.softmax(x, axis=axis)

def _gelu(x):
    return jax.nn.gelu(x, approximate=True)

def _silu(x):
    return jax.nn.silu(x)

def _sigmoid(x):
    return jax.nn.sigmoid(x)

def _layernorm(x, axis=-1, eps=1e-05):
    m = jnp.mean(x, axis=axis, keepdims=True)
    v = jnp.var(x, axis=axis, keepdims=True)
    return (x - m) / jnp.sqrt(v + eps)

def _scatter_add(tgt, idx, src, axis=0):
    return tgt.at[idx].add(src)

def _segment_sum(src, seg, n):
    return jax.ops.segment_sum(src, seg, n)
kernel_name = 'mk_cond_resid_d1_seqx_r2_bb4d94'

def setup_inputs(seed: int=0):
    np.random.seed(seed)
    _w = jnp.asarray

    def _rec_inputs():
        import jax
        import jax.numpy as jnp
        _rk = jax.random.key(seed)
        x = -0.0002928 + 1 * jax.random.normal(jax.random.fold_in(_rk, 1), (64, 128, 512), jnp.float32)
        _lenS = 128 - jax.random.randint(jax.random.fold_in(_rk, 7), (64,), 0, max(1, 128 // 4) + 1, jnp.int32)
        _lenS2 = 128 - jax.random.randint(jax.random.fold_in(_rk, 8), (64,), 0, max(1, 128 // 4) + 1, jnp.int32)
        fside_16xSxS_0 = -5.72187e-05 + 0.999849 * jax.random.normal(jax.random.fold_in(_rk, 11), (16, 128, 128), jnp.float32)
        cond_64 = -0.0265395 + 0.99382 * jax.random.normal(jax.random.fold_in(_rk, 13), (64, 64), jnp.float32)
        _validS = jnp.arange(128)[None, :] < _lenS[:, None]
        _validS2 = jnp.arange(128)[None, :] < _lenS2[:, None]
        _causal = jnp.tril(jnp.ones((128, 128), dtype=bool))
        mask_BxS_bk0 = jnp.logical_not(jnp.broadcast_to(_validS[:, :], (64, 128)))
        return (x, fside_16xSxS_0, cond_64, mask_BxS_bk0)
    x, fside_16xSxS_0, cond_64, mask_BxS_bk0 = _rec_inputs()

    def _L0_cond_setup():
        import jax, jax.numpy as jnp
        import numpy as np
        B, N, DIM, H, DH = (2, 1024, 512, 16, 64)
        INNER = H * DH
        EPS = 1e-05

        def layernorm(x, g):
            mean = jnp.mean(x, axis=-1, keepdims=True)
            var = jnp.var(x, axis=-1, keepdims=True)
            return (x - mean) * jax.lax.rsqrt(var + EPS) * g
        key = jax.random.key(seed)
        ks = jax.random.split(key, 10)
        x = jax.random.normal(ks[0], (B, N, DIM), dtype=jnp.float32)
        attn_bias = jax.random.normal(ks[1], (H, N, N), dtype=jnp.float32)
        mask = jax.random.randint(ks[2], (B, N), 0, 2).astype(bool)
        g_in = jnp.ones((DIM,), dtype=jnp.float32)
        null_attn_bias = jax.random.normal(ks[3], (H,), dtype=jnp.float32)
        null_kv = jax.random.normal(ks[4], (2, DH), dtype=jnp.float32)
        Wq = jax.random.normal(ks[5], (DIM, INNER), dtype=jnp.float32) * 0.02
        Wkv = jax.random.normal(ks[6], (DIM, 2 * DH), dtype=jnp.float32) * 0.02
        Wo = jax.random.normal(ks[7], (INNER, DIM), dtype=jnp.float32) * 0.02
        g_out = jnp.ones((DIM,), dtype=jnp.float32)
        return {'x': x, 'attn_bias': attn_bias, 'mask': mask, 'g_in': g_in, 'null_attn_bias': null_attn_bias, 'null_kv': null_kv, 'Wq': Wq, 'Wkv': Wkv, 'Wo': Wo, 'g_out': g_out}
    _L0_cond_all = _L0_cond_setup()
    _L0_cond_in = {k: v for k, v in _L0_cond_all.items() if k in ('g_in', 'null_attn_bias', 'Wq', 'Wkv', 'Wo', 'g_out')}
    del _L0_cond_all
    return {'x': x, 'fside_16xSxS_0': fside_16xSxS_0, 'cond_64': cond_64, 'mask_BxS_bk0': mask_BxS_bk0, 'L0_cond_g_in': _L0_cond_in['g_in'], 'L0_cond_null_attn_bias': _L0_cond_in['null_attn_bias'], 'L0_cond_Wq': _L0_cond_in['Wq'], 'L0_cond_Wkv': _L0_cond_in['Wkv'], 'L0_cond_Wo': _L0_cond_in['Wo'], 'L0_cond_g_out': _L0_cond_in['g_out']}

def reference(x, fside_16xSxS_0, cond_64, mask_BxS_bk0, L0_cond_g_in, L0_cond_null_attn_bias, L0_cond_Wq, L0_cond_Wkv, L0_cond_Wo, L0_cond_g_out):
    import jax
    import jax.numpy as jnp

    def _L0_cond_ref(x, attn_bias, mask, g_in, null_attn_bias, null_kv, Wq, Wkv, Wo, g_out):
        import jax, jax.numpy as jnp
        import numpy as np
        B, N, DIM, H, DH = (2, 1024, 512, 16, 64)
        INNER = H * DH
        EPS = 1e-05

        def layernorm(x, g):
            mean = jnp.mean(x, axis=-1, keepdims=True)
            var = jnp.var(x, axis=-1, keepdims=True)
            return (x - mean) * jax.lax.rsqrt(var + EPS) * g
        b, n, _ = x.shape
        scale = DH ** (-0.5)
        xn = layernorm(x, g_in)
        q = (xn @ Wq).reshape(b, n, H, DH).transpose(0, 2, 1, 3) * scale
        kv = xn @ Wkv
        k, v = (kv[..., :DH], kv[..., DH:])
        nk = jnp.broadcast_to(null_kv[0], (b, 1, DH))
        nv = jnp.broadcast_to(null_kv[1], (b, 1, DH))
        k = jnp.concatenate([nk, k], axis=1)
        v = jnp.concatenate([nv, v], axis=1)
        sim = jnp.einsum('bhid,bjd->bhij', q, k)
        null_col = jnp.broadcast_to(null_attn_bias[:, None, None], (H, n, 1))
        bias = jnp.concatenate([null_col, attn_bias], axis=-1)
        sim = sim + bias
        neg = -jnp.finfo(sim.dtype).max
        j = n + 1
        causal_mask = jnp.triu(jnp.ones((n, j), dtype=bool), k=j - n + 1)
        sim = jnp.where(causal_mask, neg, sim)
        mask_p = jnp.pad(mask, ((0, 0), (1, 0)), constant_values=True)
        sim = jnp.where(mask_p[:, None, None, :], sim, neg)
        attn = jax.nn.softmax(sim, axis=-1)
        out = jnp.einsum('bhij,bjd->bhid', attn, v)
        out = out.transpose(0, 2, 1, 3).reshape(b, n, INNER)
        out = out @ Wo
        return layernorm(out, g_out)
    x = x + _L0_cond_ref(x, fside_16xSxS_0, mask_BxS_bk0, L0_cond_g_in, L0_cond_null_attn_bias, cond_64, L0_cond_Wq, L0_cond_Wkv, L0_cond_Wo, L0_cond_g_out)
    return x

_drawn_inputs = setup_inputs


def setup_inputs(seed=0):
    import zlib

    import numpy as np

    out = dict(_drawn_inputs(seed))
    spreads = {'L0_cond_g_in': (1.0, 0.2), 'L0_cond_g_out': (1.0, 0.2)}
    factors = {}
    for name, (base, spread) in spreads.items():
        noise = np.random.default_rng([zlib.crc32(name.encode()), seed]).standard_normal(out[name].shape)
        drawn = base * np.exp(spread * noise) if base else spread * noise
        out[name] = jnp.asarray(drawn.astype(out[name].dtype))
    for name, factor in factors.items():
        out[name] = (out[name] * factor).astype(out[name].dtype)
    return out
```

```python
from contextlib import ExitStack

import concourse.bass as bass
from concourse import mybir

F32 = mybir.dt.float32
F32R = mybir.dt.float32r
U8 = mybir.dt.uint8
ALU = mybir.AluOpType
ACT = mybir.ActivationFunctionType

P = 128
B, N, DIM = 64, 128, 512
H, DH = 16, 64
INNER = H * DH
EPS = 1e-5
SCALE = DH ** -0.5
MASKED = 1e38

KT = DIM // P
OT = INNER // P
GB = 2
TOK = GB * N
GROUPS = B // GB
HC = 4
CB = H // HC
CG = GB * CB
PAIRS = GROUPS // 2
CP = 2 * CG
QT = INNER // P
LAG_W, LAG_O = 2, 3

FRONT = {
    0: [("x", 0), ("x", 1), ("x", 2), ("x", 3)],
    1: [("kv", 0), ("q", 0)],
    2: [("v", 0), ("q", 1)],
    3: [("q", 2)],
    4: [("q", 3)],
    5: [("q", 4)],
    6: [("q", 5), ("q", 6)],
    7: [("q", 7)],
}
USE = {part: j for j, part in enumerate(part for parts in FRONT.values() for part in parts)}
USES = len(USE)
STEP_STATS, STEP_XN = 4, 6
STEP_OUT_STATS = 3
STEP_OUT_NORM = 0


def attention_block(nc, x, attn_bias, null_kv, mask, g_in, null_bias, wq, wkv, wo, g_out, out):
    x_pairs = x.rearrange("(q r) p d -> q p r d", r=2 * GB)
    out_pairs = out.rearrange("(q r) p d -> q p r d", r=2 * GB)
    mask_pairs = mask.rearrange("(q r) n -> q (r n)", r=2 * GB)

    with ExitStack() as ctx:
        def sb(name, shape, dt=F32):
            return ctx.enter_context(nc.sbuf_tensor(name, shape, dt))

        def psum(name, shape):
            return ctx.enter_context(nc.psum_tensor(name, shape, F32))

        def sem(name):
            return ctx.enter_context(nc.semaphore(name))

        ident = sb("ident", [P, P])
        wq_hi, wq_lo = sb("wq_hi", [P, KT, INNER], F32R), sb("wq_lo", [P, KT, INNER], F32R)
        wkv_hi, wkv_lo = sb("wkv_hi", [P, KT, 2 * DH], F32R), sb("wkv_lo", [P, KT, 2 * DH], F32R)
        wo_hi, wo_lo = sb("wo_hi", [P, OT, DIM], F32R), sb("wo_lo", [P, OT, DIM], F32R)
        w_raw = sb("w_raw", [P, KT * INNER])
        bias_c = sb("bias_c", [P, H, N])
        nb_row = sb("nb_row", [P, H])
        gin_col = sb("gin_col", [P, KT])
        gout_row = sb("gout_row", [P, DIM])
        nk_col = sb("nk_col", [DH, 1])
        nv_col = sb("nv_col", [P, 1])
        eps_col = sb("eps_col", [P, 2])
        pow_col = sb("pow_col", [P, 2])
        x_in = sb("x_in", [P, 2, GB, DIM])
        x_res = sb("x_res", [P, 2, GB, DIM])
        mask_u8 = sb("mask_u8", [P, 2, GB, N], U8)
        mask_add = sb("mask_add", [P, 2, GB, N])
        x_stats = sb("x_stats", [P, GB, 6])
        x_mv = sb("x_mv", [P, GB, 2])
        x_var = sb("x_var", [P, GB])
        x_rstd = sb("x_rstd", [P, GB])
        xn = sb("xn", [P, GB, DIM])
        xt_hi, xt_lo = sb("xt_hi", [P, KT, TOK], F32R), sb("xt_lo", [P, KT, TOK], F32R)
        k_raw = sb("k_raw", [DH, TOK])
        v_raw = sb("v_raw", [P, TOK])
        keys = sb("keys", [P, 2, GB, 2, N], F32R)
        v_hi, v_lo = sb("v_hi", [P, 2, GB, 3 * DH], F32R), sb("v_lo", [P, 2, GB, 3 * DH], F32R)
        q_sb = sb("q_sb", [P, 2, H, TOK], F32R)
        bias_b = sb("bias_b", [P, 2, HC, N])
        s_low = sb("s_low", [P, 2, 2, N])
        logit = sb("logit", [P, 2, HC, N + 1])
        neg_max = sb("neg_max", [P, 2, HC])
        w_exp = sb("w_exp", [P, 2, HC, N + 1])
        w_sum = sb("w_sum", [P, 2, HC])
        w_inv = sb("w_inv", [P, 2, HC])
        w_nrm = sb("w_nrm", [P, 2, HC, N])
        wt_hi, wt_lo = sb("wt_hi", [P, 2, HC, N], F32R), sb("wt_lo", [P, 2, HC, N], F32R)
        o_hi, o_lo = sb("o_hi", [P, 2, 2, N], F32R), sb("o_lo", [P, 2, 2, N], F32R)
        y_stats = sb("y_stats", [P, 2, 6])
        y_mv = sb("y_mv", [P, 2, 2])
        y_var = sb("y_var", [P, 2])
        y_rstd = sb("y_rstd", [P, 2])
        y_shift = sb("y_shift", [P, 2])
        y_nrm = sb("y_nrm", [P, 2, DIM])
        y_out = sb("y_out", [P, 2, DIM])

        ps_s = [psum(f"ps_s{i}", [P, 2, 2, N]) for i in range(2)]
        ps_wt = psum("ps_wt", [P, HC, N])
        ps_pv = psum("ps_pv", [P, 2, N])
        ps_proj = [psum(f"ps_proj{i}", [P, 512]) for i in range(2)]
        ps_o = [psum(f"ps_o{i}", [P, DIM]) for i in range(2)]

        ld_const = sem("ld_const")
        ld_wkv, ld_wq, ld_wo = sem("ld_wkv"), sem("ld_wq"), sem("ld_wo")
        ld_bias = sem("ld_bias")
        ld_x = [sem(f"ld_x{i}") for i in range(2)]
        ld_mask = [sem(f"ld_mask{i}") for i in range(2)]
        x_copied = [sem(f"x_copied{i}") for i in range(2)]
        stored = [sem(f"stored{i}") for i in range(2)]
        ident_zero, ident_made = sem("ident_zero"), sem("ident_made")
        filled = sem("filled")
        waits_taken = sem("waits_taken")
        w_hi_made, w_lo_made = sem("w_hi_made"), sem("w_lo_made")
        bias_shifted, bias_made = sem("bias_shifted"), sem("bias_made")
        mask_made = sem("mask_made")
        x_stat_made, x_mv_made, x_var_made, x_rstd_made = (sem("x_stat_made"), sem("x_mv_made"),
                                                           sem("x_var_made"), sem("x_rstd_made"))
        xn_made = sem("xn_made")
        proj_done = sem("proj_done")
        proj_read = sem("proj_read")
        xt_hi_made = sem("xt_hi_made")
        k_raw_made, v_raw_made = sem("k_raw_made"), sem("v_raw_made")
        k_hi_made, k_lo_made = sem("k_hi_made"), sem("k_lo_made")
        v_hi_made = sem("v_hi_made")
        q_hi_made = sem("q_hi_made")
        s_done, s_low_made, s_read = sem("s_done"), sem("s_low_made"), sem("s_read")
        bias_b_made = sem("bias_b_made")
        exp_made, inv_made, nrm_made = sem("exp_made"), sem("inv_made"), sem("nrm_made")
        wt_done, wt_hi_made, wt_lo_made = sem("wt_done"), sem("wt_hi_made"), sem("wt_lo_made")
        pv_done, o_hi_made, o_lo_made = sem("pv_done"), sem("o_hi_made"), sem("o_lo_made")
        o_done = sem("o_done")
        y_stat_made, y_mv_made, y_var_made, y_rstd_made, y_shift_made = (
            sem("y_stat_made"), sem("y_mv_made"), sem("y_var_made"), sem("y_rstd_made"), sem("y_shift_made"))
        y_nrm_made, y_g_made, y_out_made = sem("y_nrm_made"), sem("y_g_made"), sem("y_out_made")

        CONST_LOADS = 8

        def wait(eng, s, value):
            if isinstance(value, int) and value <= 0:
                return
            eng.wait_ge(s, value)

        def apart(eng):
            eng.sem_inc(waits_taken, 1)

        def run_pairs(eng, body):
            body(0, True, False)
            with eng.Fori(1, PAIRS - 1) as p:
                body(p, False, False)
            body(PAIRS - 1, False, True)

        def has_front(t, last):
            return not (last and t >= CG)

        block = ctx.enter_context(nc.Block())

        @block.sync
        def _(sp):
            def copy_x(q, k):
                sp.wait_ge(ld_x[k], 16 * (q + 1))
                apart(sp)
                sp.dma_start(x_res[:, k], x_in[:, k]).then_inc(x_copied[k], 16)

            def reload_x(q, k):
                sp.wait_ge(x_copied[k], 16 * q)
                apart(sp)
                sp.wait_ge(xn_made, GB * (2 * q + k - 1))
                apart(sp)
                sp.wait_ge(mask_made, 2 * q + k - 1)
                apart(sp)
                load_x(q, k)

            def load_x(q, k):
                sp.dma_start(x_in[:, k], x_pairs[q, :, GB * k:GB * (k + 1), :]).then_inc(ld_x[k], 16)
                sp.dma_start(mask_u8[:, k].rearrange("p b n -> p (b n)"),
                             mask_pairs[q, TOK * k:TOK * (k + 1)].partition_broadcast(P)).then_inc(ld_mask[k], 16)

            sp.dma_start(gin_col[:], g_in.rearrange("(k p) -> p k", p=P),
                         allow_slow_non_contiguous=True).then_inc(ld_const, 16)
            load_x(0, 0)
            sp.dma_start(w_raw[:, 0:KT * 2 * DH].rearrange("p (k n) -> p k n", k=KT),
                         wkv.rearrange("(k p) n -> p k n", p=P)).then_inc(ld_wkv, 16)
            load_x(0, 1)
            sp.dma_start(gout_row[:], g_out.partition_broadcast(P)).then_inc(ld_const, 16)
            sp.dma_start(nb_row[:], null_bias.partition_broadcast(P)).then_inc(ld_const, 16)
            sp.dma_start(nk_col[:], null_kv[0].rearrange("(d o) -> d o", o=1)).then_inc(ld_const, 16)
            sp.dma_start(nv_col[0:DH], null_kv[1].rearrange("(d o) -> d o", o=1)).then_inc(ld_const, 16)
            sp.dma_start(nv_col[DH:P], null_kv[1].rearrange("(d o) -> d o", o=1)).then_inc(ld_const, 16)
            sp.dma_start(bias_c[:], attn_bias.rearrange("h i j -> i h j")).then_inc(ld_bias, 16)
            sp.wait_ge(w_lo_made, 1)
            sp.dma_start(w_raw[:].rearrange("p (k n) -> p k n", k=KT),
                         wq.rearrange("(k p) n -> p k n", p=P)).then_inc(ld_wq, 16)
            sp.wait_ge(w_lo_made, 2)
            sp.dma_start(w_raw[:].rearrange("p (k n) -> p k n", k=OT),
                         wo.rearrange("(k p) n -> p k n", p=P)).then_inc(ld_wo, 16)

            for k in range(2):
                copy_x(0, k)
            for k in range(2):
                reload_x(1, k)

            def body(p, copies, loads):
                for k in range(2):
                    for b in range(GB):
                        sp.wait_ge(y_out_made, GB * (2 * p + k) + b + 1)
                        apart(sp)
                        sp.dma_start(out_pairs[p, :, GB * k + b, :], y_out[:, b]).then_inc(stored[b], 16)
                    if copies:
                        copy_x(p + 1, k)
                    if loads:
                        reload_x(p + 2, k)

            with sp.Fori(0, PAIRS - 2) as p:
                body(p, True, True)
            body(PAIRS - 2, True, False)
            body(PAIRS - 1, False, False)
            for b in range(GB):
                sp.wait_ge(stored[b], 16 * GROUPS)

        @block.tensor
        def _(pe):
            def scores(n, g, t):
                b, c, slot = t // CB % GB, t % CB, t // CG
                if b == 0:
                    wait(pe, proj_read, USES * g + USE["q", HC // 2 * (c + 1) - 1] + 1)
                    if c == 0:
                        wait(pe, k_lo_made, g + 1)
                for u in range(2):
                    wait(pe, s_read, 2 * n + u - 1)
                    for i in range(2):
                        h = HC * c + 2 * u + i
                        mm = pe.matmul(ps_s[u][:, i].rearrange("p a n -> p (a n)"), q_sb[:, slot, h, N * b:N * (b + 1)],
                                       keys[:, slot, b].rearrange("p a n -> p (a n)"), start=True, stop=True)
                    mm.then_inc(s_done, 1)

            def weights_t(n, t):
                s = t % 2
                wait(pe, nrm_made, n + 1)
                wait(pe, wt_lo_made, n)
                for i in range(HC):
                    mm = pe.transpose(ps_wt[:, i], w_nrm[:, s, i], ident[:])
                mm.then_inc(wt_done, 1)

            def values(n, g, t):
                b, s, slot = t // CB % GB, t % 2, t // CG % 2
                wait(pe, wt_lo_made, n + 1)
                wait(pe, o_lo_made, n)
                if t % CG == 0:
                    wait(pe, proj_read, USES * g + USE["v", 0] + 1)
                even, odd = slice(DH, 3 * DH), slice(0, 2 * DH)
                todo = [(v, w, par) for v, w in ((v_hi, wt_hi), (v_lo, wt_hi), (v_hi, wt_lo)) for par in range(2)]
                for j, (v, w, par) in enumerate(todo):
                    mm = pe.matmul(ps_pv[:], v[:, slot, b, odd if par else even], w[:, s, par::2],
                                   start=(j == 0), stop=(j == len(todo) - 1))
                mm.then_inc(pv_done, 1)

            def project_out(n, batch, t):
                b, c, s = t // CB % GB, t % CB, t % 2
                wait(pe, o_lo_made, n + 1)
                if c == 0:
                    wait(pe, y_nrm_made, batch - 1)
                todo = [(o, w, i) for i in range(2) for o, w in ((o_hi, wo_hi), (o_hi, wo_lo), (o_lo, wo_hi))]
                for j, (o, w, i) in enumerate(todo):
                    mm = pe.matmul(ps_o[b][:], o[:, s, i], w[:, 2 * c + i],
                                   start=(c == 0 and j == 0), stop=(c == CB - 1 and j == len(todo) - 1))
                mm.then_inc(o_done, 1)

            def project(ps, f, w_hi, w_lo, cols):
                todo = [(k, w, xt) for k in range(KT) for w, xt in ((w_hi, xt_hi), (w_lo, xt_hi), (w_hi, xt_lo))]
                for j, (k, w, xt) in enumerate(todo):
                    mm = pe.matmul(ps[:, 0:TOK], w[:, k, cols], xt[:, k], start=(j == 0), stop=(j == len(todo) - 1))
                return mm

            def front(f, kind, i):
                use = USE[kind, i]
                ps = ps_proj[use % 2]
                wait(pe, proj_read, USES * f + use - 1)
                if kind == "x":
                    if i == 0:
                        wait(pe, xn_made, GB * (f + 1))
                    for b in range(GB):
                        mm = pe.transpose(ps[:, N * b:N * (b + 1)], xn[:, b, P * i:P * (i + 1)], ident[:])
                elif kind == "kv":
                    wait(pe, proj_read, USES * f + KT)
                    mm = project(ps, f, wkv_hi, wkv_lo, slice(0, 2 * DH))
                elif kind == "v":
                    wait(pe, v_raw_made, f + 1)
                    apart(pe)
                    for b in range(GB):
                        mm = pe.transpose(ps[:, DH * b:DH * (b + 1)], v_raw[DH:P, N * b:N * (b + 1)], ident[DH:P, DH:P])
                else:
                    mm = project(ps, f, wq_hi, wq_lo, slice(P * i, P * (i + 1)))
                mm.then_inc(proj_done, 1)

            pe.wait_ge(ident_made, 1)
            for kinds in FRONT.values():
                for kind, i in kinds:
                    if kind == "kv":
                        pe.wait_ge(w_lo_made, 1)
                    if kind == "q" and i == 0:
                        pe.wait_ge(w_lo_made, 2)
                    front(0, kind, i)

            def body(p, first, last):
                for t in range(CP):
                    n, g = CP * p + t, 2 * p + t // CG
                    scores(n, g, t)
                    if not (first and t < LAG_W):
                        weights_t(n - LAG_W, t - LAG_W)
                    if has_front(t, last):
                        for kind, i in FRONT[t % CG]:
                            front(g + 1, kind, i)
                    if not (first and t < LAG_W):
                        values(n - LAG_W, 2 * p + (t - LAG_W) // CG, (t - LAG_W) % CP)
                    if first and t == LAG_O:
                        pe.wait_ge(w_lo_made, 3)
                    if not (first and t < LAG_O):
                        project_out(n - LAG_O, GB * 2 * p + (t - LAG_O) // CB, (t - LAG_O) % CP)

            run_pairs(pe, body)
            end = CP * PAIRS
            for n in range(end, end + LAG_O):
                if n < end + LAG_W:
                    weights_t(n - LAG_W, n - LAG_W)
                    values(n - LAG_W, GROUPS - 1, (n - LAG_W) % CP)
                project_out(n - LAG_O, B - 1, (n - LAG_O) % CP)

        @block.vector
        def _(dve):
            def logits(n, g, t):
                b, c, s = t // CB % GB, t % CB, t % 2
                wait(dve, bias_b_made, n + 1)
                for u in range(2):
                    wait(dve, s_done, 2 * n + u + 1)
                    wait(dve, s_read, 2 * n + u - 1)
                    nc.vector.tensor_tensor(s_low[:, u], ps_s[u][:, :, 1], bias_b[:, s, 2 * u:2 * u + 2],
                                            ALU.add).then_inc(s_low_made, 1)
                wait(dve, exp_made, n - 1)
                for u in range(2):
                    wait(dve, s_low_made, 2 * n + u + 1)
                    apart(dve)
                    for i in range(2):
                        j = 2 * u + i
                        ins = nc.vector.tensor_tensor_reduce(
                            logit[:, s, j, 0:N], ps_s[u][:, i, 0], s_low[:, u, i], -1.0, 0.0, ALU.add, ALU.min,
                            neg_max[:, s, j:j + 1])
                    ins.then_inc(s_read, 1)

            def inverse(n, t):
                s = t % 2
                wait(dve, exp_made, n + 1)
                wait(dve, nrm_made, n - 1)
                nc.vector.reciprocal(w_inv[:, s], w_sum[:, s]).then_inc(inv_made, 1)

            def weights_lo(n, t):
                s = t % 2
                wait(dve, wt_hi_made, n + 1)
                wait(dve, pv_done, n - 1)
                nc.vector.tensor_tensor(wt_lo[:, s], ps_wt[:], wt_hi[:, s].bitcast(F32),
                                        ALU.subtract).then_inc(wt_lo_made, 1)

            def heads_lo(n, t):
                s = t % 2
                wait(dve, o_hi_made, n + 1)
                wait(dve, o_done, n - 1)
                nc.vector.scalar_tensor_tensor(out=o_lo[:, s], in0=ps_pv[:], scalar=nv_col[:, 0:1],
                                               in1=o_hi[:, s].bitcast(F32), op0=ALU.add,
                                               op1=ALU.subtract).then_inc(o_lo_made, 1)

            def out_stats(batch, t):
                b = t // CB % GB
                wait(dve, o_done, CB * (batch + 1))
                wait(dve, y_mv_made, batch)
                nc.vector.bn_stats(y_stats[:, b], ps_o[b][:]).then_inc(y_stat_made, 1)
                wait(dve, y_stat_made, batch + 1)
                wait(dve, y_shift_made, batch - 1)
                apart(dve)
                nc.vector.bn_aggr(y_mv[:, b], y_stats[:, b]).then_inc(y_mv_made, 1)

            def x_stats_of(f, k):
                wait(dve, ld_x[k], 8 * (f - k) + 16)
                for b in range(GB):
                    wait(dve, x_mv_made, GB * f + b - 1)
                    nc.vector.bn_stats(x_stats[:, b], x_in[:, k, b]).then_inc(x_stat_made, 1)
                wait(dve, x_rstd_made, f)
                wait(dve, xn_made, GB * f)
                for b in range(GB):
                    wait(dve, x_stat_made, GB * f + b + 1)
                    apart(dve)
                    nc.vector.bn_aggr(x_mv[:, b], x_stats[:, b]).then_inc(x_mv_made, 1)

            def x_norm(f, k):
                wait(dve, x_rstd_made, f + 1)
                wait(dve, x_mv_made, GB * (f + 1))
                wait(dve, proj_done, USES * (f - 1) + KT)
                for b in range(GB):
                    nc.vector.tensor_scalar(xn[:, b], x_in[:, k, b], x_mv[:, b, 0:1], x_rstd[:, b:b + 1],
                                            ALU.subtract, ALU.mult).then_inc(xn_made, 1)
                wait(dve, ld_mask[k], 8 * (f - k) + 16)
                wait(dve, bias_b_made, CG * (f - 1))
                nc.vector.tensor_scalar(mask_add[:, k], mask_u8[:, k], MASKED, -MASKED, ALU.mult,
                                        ALU.add).then_inc(mask_made, 1)

            def front(f, slot, kind, i):
                use = USE[kind, i]
                ps = ps_proj[use % 2]
                if kind == "x":
                    wait(dve, xt_hi_made, KT * f + i + 1)
                    nc.vector.scalar_tensor_tensor(out=xt_lo[:, i], in0=ps[:, 0:TOK], scalar=gin_col[:, i:i + 1],
                                                   in1=xt_hi[:, i].bitcast(F32), op0=ALU.mult,
                                                   op1=ALU.subtract).then_inc(proj_read, 1)
                elif kind == "kv":
                    wait(dve, proj_done, USES * f + use + 1)
                    wait(dve, k_lo_made, f)
                    wait(dve, k_hi_made, 2 * f)
                    nc.vector.tensor_scalar(k_raw[:], ps[0:DH, 0:TOK], nk_col[:, 0:1], SCALE, ALU.subtract,
                                            ALU.mult).then_inc(k_raw_made, 1)
                    wait(dve, proj_done, USES * (f - 1) + USE["v", 0] + 1)
                    nc.vector.tensor_scalar(v_raw[DH:P, :], ps[DH:P, 0:TOK], nv_col[DH:P, 0:1], None,
                                            ALU.subtract).then_inc(v_raw_made, 1)
                    wait(dve, v_raw_made, f + 1)
                    wait(dve, k_raw_made, f + 1)
                    dve.sem_inc(proj_read, 1)
                    wait(dve, k_hi_made, 2 * f + 2)
                    for half in range(2):
                        ins = nc.vector.tensor_tensor(
                            keys[DH * half:DH * (half + 1), slot, :, 1], k_raw[:].rearrange("p (b n) -> p b n", b=GB),
                            keys[0:DH, slot, :, 0].bitcast(F32), ALU.subtract)
                    ins.then_inc(k_lo_made, 1)
                elif kind == "v":
                    wait(dve, v_hi_made, f + 1)
                    nc.vector.tensor_tensor(v_lo[:, slot, :, DH:2 * DH],
                                            ps[:, 0:GB * DH].rearrange("p (b d) -> p b d", b=GB),
                                            v_hi[:, slot, :, DH:2 * DH].bitcast(F32), ALU.subtract
                                            ).then_inc(proj_read, 1)
                else:
                    for half in range(2):
                        up, across = slice(DH * half, DH * (half + 1)), slice(DH * (1 - half), DH * (2 - half))
                        wait(dve, q_hi_made, 2 * QT * f + 2 * i + half + 1)
                        ins = nc.vector.tensor_tensor(q_sb[across, slot, 2 * i + half], ps[up, 0:TOK],
                                                      q_sb[up, slot, 2 * i + half].bitcast(F32), ALU.subtract)
                    ins.then_inc(proj_read, 1)

            for z in (v_hi, v_lo):
                nc.vector.memset(z[:, :, :, 0:DH].bitcast(F32), 0.0)
                nc.vector.memset(z[:, :, :, 2 * DH:3 * DH].bitcast(F32), 0.0)
            nc.vector.memset(eps_col[:], EPS)
            nc.vector.memset(pow_col[:], -0.5)
            nc.vector.memset(logit[:, :, :, N:N + 1], 0.0).then_inc(filled, 1)
            x_stats_of(0, 0)
            x_norm(0, 0)
            dve.wait_ge(ld_wkv, 16)
            dve.wait_ge(w_hi_made, 1)
            nc.vector.tensor_tensor(wkv_lo[:].rearrange("p k n -> p (k n)"), w_raw[:, 0:KT * 2 * DH],
                                    wkv_hi[:].rearrange("p k n -> p (k n)").bitcast(F32),
                                    ALU.subtract).then_inc(w_lo_made, 1)
            dve.wait_ge(ld_const, 16 * 6)
            for i in range(KT):
                front(0, 0, "x", i)
            x_stats_of(1, 1)
            x_norm(1, 1)
            front(0, 0, "kv", 0)
            dve.wait_ge(ld_bias, 16)
            nc.vector.tensor_tensor(bias_c[:], bias_c[:], nb_row[:].unsqueeze(2).to_broadcast([P, H, N]),
                                    ALU.subtract).then_inc(bias_shifted, 1)
            dve.wait_ge(w_hi_made, 2)
            nc.vector.tensor_tensor(wq_lo[:].rearrange("p k n -> p (k n)"), w_raw[:],
                                    wq_hi[:].rearrange("p k n -> p (k n)").bitcast(F32),
                                    ALU.subtract).then_inc(w_lo_made, 1)
            for kind, i in list(USE)[KT + 1:]:
                front(0, 0, kind, i)
            dve.wait_ge(w_hi_made, 3)
            nc.vector.tensor_tensor(wo_lo[:].rearrange("p k n -> p (k n)"), w_raw[:],
                                    wo_hi[:].rearrange("p k n -> p (k n)").bitcast(F32),
                                    ALU.subtract).then_inc(w_lo_made, 1)

            def body(p, first, last):
                for t in range(CP):
                    n, g = CP * p + t, 2 * p + t // CG
                    logits(n, g, t)
                    if not (first and t < LAG_W):
                        weights_lo(n - LAG_W, t - LAG_W)
                    inverse(n, t)
                    if has_front(t, last):
                        for kind, i in FRONT[t % CG]:
                            front(g + 1, (t // CG + 1) % 2, kind, i)
                    if not (first and t < LAG_W):
                        heads_lo(n - LAG_W, t - LAG_W)
                    if t % CB == STEP_OUT_STATS and not (first and t < CB):
                        out_stats(2 * GB * p + t // CB - 1, (t - CB) % CP)
                    if not last:
                        if t % CG == STEP_STATS:
                            x_stats_of(g + 2, t // CG)
                        if t % CG == STEP_XN:
                            x_norm(g + 2, t // CG)

            run_pairs(dve, body)
            end = CP * PAIRS
            for n in range(end, end + LAG_W):
                weights_lo(n - LAG_W, n)
                heads_lo(n - LAG_W, n)
            out_stats(B - 1, CP - 1)

        @block.scalar
        def _(act):
            def weights_hi(n, t):
                s = t % 2
                wait(act, wt_done, n + 1)
                wait(act, pv_done, n - 1)
                nc.scalar.copy(wt_hi[:, s], ps_wt[:]).then_inc(wt_hi_made, 1)

            def exponentials(n, t):
                s = t % 2
                wait(act, nrm_made, n - 1)
                wait(act, inv_made, n - 1)
                for j in range(HC):
                    if j % 2 == 0:
                        wait(act, s_read, 2 * n + j // 2 + 1)
                    ins = nc.scalar.activation(w_exp[:, s, j], logit[:, s, j], ACT.Exp, bias=neg_max[:, s, j:j + 1],
                                               scale=-1.0, accum_out=w_sum[:, s, j:j + 1])
                ins.then_inc(exp_made, 1)

            def heads_hi(n, t):
                s = t % 2
                wait(act, pv_done, n + 1)
                wait(act, o_done, n - 1)
                nc.scalar.activation(o_hi[:, s], ps_pv[:], ACT.Identity, bias=nv_col[:, 0:1]).then_inc(o_hi_made, 1)

            def out_norm(batch, t):
                b = t // CB % GB
                wait(act, y_shift_made, batch + 1)
                wait(act, y_out_made, batch - 1)
                nc.scalar.activation(y_nrm[:, b], ps_o[b][:], ACT.Identity, bias=y_shift[:, b:b + 1],
                                     scale=y_rstd[:, b:b + 1]).then_inc(y_nrm_made, 1)

            def front(f, slot, kind, i):
                use = USE[kind, i]
                ps = ps_proj[use % 2]
                if kind == "x":
                    wait(act, proj_done, USES * f + use + 1)
                    nc.scalar.activation(xt_hi[:, i], ps[:, 0:TOK], ACT.Copy,
                                         scale=gin_col[:, i:i + 1]).then_inc(xt_hi_made, 1)
                elif kind == "kv":
                    wait(act, k_raw_made, f + 1)
                    for half in range(2):
                        nc.scalar.copy(keys[DH * half:DH * (half + 1), slot, :, 0],
                                       k_raw[:].rearrange("p (b n) -> p b n", b=GB)).then_inc(k_hi_made, 1)
                elif kind == "v":
                    wait(act, proj_done, USES * f + use + 1)
                    nc.scalar.copy(v_hi[:, slot, :, DH:2 * DH],
                                   ps[:, 0:GB * DH].rearrange("p (b d) -> p b d", b=GB)).then_inc(v_hi_made, 1)
                else:
                    wait(act, proj_done, USES * f + use + 1)
                    for half in range(2):
                        up = slice(DH * half, DH * (half + 1))
                        nc.scalar.copy(q_sb[up, slot, 2 * i + half], ps[up, 0:TOK]).then_inc(q_hi_made, 1)

            act.wait_ge(ld_wkv, 16)
            nc.scalar.copy(wkv_hi[:].rearrange("p k n -> p (k n)"), w_raw[:, 0:KT * 2 * DH]).then_inc(w_hi_made, 1)
            act.wait_ge(ld_const, 16 * 6)
            for i in range(KT):
                front(0, 0, "x", i)
            front(0, 0, "kv", 0)
            act.wait_ge(ld_wq, 16)
            nc.scalar.copy(wq_hi[:].rearrange("p k n -> p (k n)"), w_raw[:]).then_inc(w_hi_made, 1)
            act.wait_ge(filled, 1)
            for kind, i in list(USE)[KT + 1:]:
                front(0, 0, kind, i)
            act.wait_ge(ld_wo, 16)
            nc.scalar.copy(wo_hi[:].rearrange("p k n -> p (k n)"), w_raw[:]).then_inc(w_hi_made, 1)

            def body(p, first, last):
                for t in range(CP):
                    n, g = CP * p + t, 2 * p + t // CG
                    if not (first and t < LAG_W):
                        weights_hi(n - LAG_W, t - LAG_W)
                    if t % CB == STEP_OUT_NORM and not (first and t < 2 * CB):
                        out_norm(2 * GB * p + t // CB - 2, (t - 2 * CB) % CP)
                    exponentials(n, t)
                    if has_front(t, last):
                        for kind, i in FRONT[t % CG]:
                            front(g + 1, (t // CG + 1) % 2, kind, i)
                    if not (first and t < LAG_W):
                        heads_hi(n - LAG_W, t - LAG_W)

            run_pairs(act, body)
            end = CP * PAIRS
            for n in range(end, end + LAG_W):
                weights_hi(n - LAG_W, n)
                heads_hi(n - LAG_W, n)
            out_norm(B - 2, CP - 1 - CB)
            out_norm(B - 1, CP - 1)

        @block.gpsimd
        def _(pool):
            def masked_bias(n, g, t):
                slot, b, c, s = t // CG % 2, t // CB % GB, t % CB, t % 2
                if t % CG == 0:
                    wait(pool, mask_made, g + 1)
                wait(pool, s_low_made, 2 * (n - 1))
                nc.gpsimd.tensor_tensor(bias_b[:, s], bias_c[:, HC * c:HC * (c + 1)],
                                        mask_add[:, slot, b].unsqueeze(1).to_broadcast([P, HC, N]),
                                        ALU.add).then_inc(bias_b_made, 1)

            def normalize(n, t):
                s = t % 2
                wait(pool, inv_made, n + 1)
                wait(pool, wt_done, n - 1)
                nc.gpsimd.tensor_tensor(w_nrm[:, s], w_exp[:, s, :, 0:N],
                                        w_inv[:, s].unsqueeze(2).to_broadcast([P, HC, N]),
                                        ALU.mult).then_inc(nrm_made, 1)

            def x_rstd_of(f):
                wait(pool, x_mv_made, GB * (f + 1))
                wait(pool, x_rstd_made, f)
                nc.gpsimd.tensor_tensor(x_var[:], x_mv[:, :, 1], eps_col[:], ALU.add).then_inc(x_var_made, 1)
                wait(pool, x_var_made, f + 1)
                wait(pool, xn_made, GB * f)
                nc.gpsimd.tensor_tensor(x_rstd[:], x_var[:], pow_col[:], ALU.pow).then_inc(x_rstd_made, 1)

            def y_scale(batch, t):
                b = t // CB % GB
                c = slice(b, b + 1)
                wait(pool, y_mv_made, batch + 1)
                wait(pool, y_nrm_made, batch - 1)
                nc.gpsimd.tensor_tensor(y_var[:, c], y_mv[:, b, 1:2], eps_col[:, 0:1], ALU.add).then_inc(y_var_made, 1)
                wait(pool, y_var_made, batch + 1)
                nc.gpsimd.tensor_tensor(y_rstd[:, c], y_var[:, c], pow_col[:, 0:1], ALU.pow).then_inc(y_rstd_made, 1)
                wait(pool, y_rstd_made, batch + 1)
                apart(pool)
                nc.gpsimd.tensor_scalar(y_shift[:, c], y_mv[:, b, 0:1], -1.0, y_rstd[:, c], ALU.mult,
                                        ALU.mult).then_inc(y_shift_made, 1)

            def residual(batch, p, t):
                slot, b = t // CG % 2, t // CB % GB
                wait(pool, y_nrm_made, batch + 1)
                nc.gpsimd.tensor_tensor(y_nrm[:, b], y_nrm[:, b], gout_row[:], ALU.mult).then_inc(y_g_made, 1)
                wait(pool, y_g_made, batch + 1)
                if b == 0:
                    wait(pool, x_copied[slot], 16 * (p + 1))
                wait(pool, stored[b], stored_before(batch, b))
                nc.gpsimd.tensor_tensor(y_out[:, b], y_nrm[:, b], x_res[:, slot, b], ALU.add).then_inc(y_out_made, 1)

            def stored_before(batch, b):
                return 8 * (batch - b)

            nc.gpsimd.memset(ident[:], 0.0).then_inc(ident_zero, 1)
            pool.wait_ge(ident_zero, 1)
            nc.gpsimd.affine_select(out=ident[:], in_=ident[:], compare_op=ALU.not_equal, fill=1.0, base=0,
                                    pattern=[[-1, P]], channel_multiplier=1).then_inc(ident_made, 1)
            pool.wait_ge(filled, 1)
            x_rstd_of(0)
            x_rstd_of(1)
            pool.wait_ge(bias_shifted, 1)
            nc.gpsimd.affine_select(out=bias_c[:], in_=bias_c[:], compare_op=ALU.is_ge, fill=-MASKED, base=0,
                                    pattern=[[0, H], [-1, N]], channel_multiplier=1).then_inc(bias_made, 1)
            pool.wait_ge(bias_made, 1)
            masked_bias(0, 0, 0)

            def body(p, first, last):
                for t in range(CP):
                    n = CP * p + t
                    if not (last and t == CP - 1):
                        masked_bias(n + 1, 2 * p + (t + 1) // CG, (t + 1) % CP)
                    if not last and t % CG == STEP_STATS:
                        x_rstd_of(2 * p + t // CG + 2)
                    normalize(n, t)
                    if t % CB == STEP_OUT_STATS and not (first and t < CB):
                        y_scale(2 * GB * p + t // CB - 1, (t - CB) % CP)
                    if t % CB == STEP_OUT_NORM and not (first and t < 2 * CB):
                        residual(2 * GB * p + t // CB - 2, p + (t - 2 * CB) // CP, (t - 2 * CB) % CP)

            run_pairs(pool, body)
            y_scale(B - 1, CP - 1)
            residual(B - 2, PAIRS - 1, CP - 1 - CB)
            residual(B - 1, PAIRS - 1, CP - 1)


_INS = ["x", "fside_16xSxS_0", "cond_64", "mask_BxS_bk0", "L0_cond_g_in", "L0_cond_null_attn_bias", "L0_cond_Wq",
        "L0_cond_Wkv", "L0_cond_Wo", "L0_cond_g_out"]


def kernel(**inputs):
    import numpy as _np
    import concourse.bacc as _bacc
    from concourse import mybir as _mybir
    from concourse.bass_utils import run_bass_kernel_spmd as _run

    nc = _bacc.Bacc("TRN2", target_bir_lowering=False, num_devices=1)
    arrays, args = {}, []
    for name in _INS:
        a = _np.ascontiguousarray(inputs[name])
        arrays[f"in_{name}_dram"] = a
        args.append(nc.dram_tensor(f"in_{name}_dram", a.shape, _mybir.dt.from_np(a.dtype), kind="ExternalInput").ap())
    out = nc.dram_tensor("out_dram", (B, N, DIM), F32, kind="ExternalOutput").ap()
    attention_block(nc, *args, out)
    r = _run(nc, [arrays], core_ids=[0])
    return r.results[0]["out_dram"]
```

```python
from contextlib import ExitStack

import concourse.bass as bass
from concourse import mybir

F32 = mybir.dt.float32
F32R = mybir.dt.float32r
U8 = mybir.dt.uint8
ALU = mybir.AluOpType
ACT = mybir.ActivationFunctionType

P = 128
B, N, DIM = 64, 128, 512
H, DH = 16, 64
INNER = H * DH
EPS = 1e-5
SCALE = DH ** -0.5
MASKED = 1e38

KT = DIM // P
KX = 2
XT = KT // KX
OT = INNER // P
GB = 2
TOK = GB * N
GROUPS = B // GB
HC = 4
CB = H // HC
CG = GB * CB
PAIRS = GROUPS // 2
CP = 2 * CG
QT = INNER // P
LAG_SUM, LAG_T, LAG_PV, LAG_HEADS, LAG_O = 1, 2, 3, 4, 5

FRONT = {
    0: [("q", 6, 0), ("q", 7, 0)],
    1: [("x", 0, 1), ("x", 1, 1)],
    2: [("kv", 0, 1)],
    3: [("q", 0, 1)],
    4: [("q", 1, 1), ("v", 0, 1)],
    5: [("q", 2, 1)],
    6: [("q", 3, 1), ("q", 4, 1)],
    7: [("q", 5, 1)],
}
STEP_K_LO = 4
USE = {part[:2]: j for j, part in enumerate(sorted((part for parts in FRONT.values() for part in parts),
                                                   key=lambda part: -part[2]))}
USES = len(USE)
STEP_STATS, STEP_XN = 4, 6
STEP_OUT_STATS, STEP_OUT_NORM, STEP_OUT_ADD = 1, 2, 3
TAIL = CB + STEP_OUT_ADD + 1


def attention_block(nc, x, attn_bias, null_kv, mask, g_in, null_bias, wq, wkv, wo, g_out, out):
    x_pairs = x.rearrange("(q r) p d -> q p r d", r=2 * GB)
    out_pairs = out.rearrange("(q r) p d -> q p r d", r=2 * GB)
    mask_pairs = mask.rearrange("(q r) n -> q (r n)", r=2 * GB)

    with ExitStack() as ctx:
        def sb(name, shape, dt=F32):
            return ctx.enter_context(nc.sbuf_tensor(name, shape, dt))

        def psum(name, shape):
            return ctx.enter_context(nc.psum_tensor(name, shape, F32))

        def sem(name):
            return ctx.enter_context(nc.semaphore(name))

        ident = sb("ident", [P, P])
        wq_hi, wq_lo = sb("wq_hi", [P, KT, INNER], F32R), sb("wq_lo", [P, KT, INNER], F32R)
        wkv_hi, wkv_lo = sb("wkv_hi", [P, KT, 2 * DH], F32R), sb("wkv_lo", [P, KT, 2 * DH], F32R)
        wo_hi, wo_lo = sb("wo_hi", [P, OT, DIM], F32R), sb("wo_lo", [P, OT, DIM], F32R)
        w_raw = sb("w_raw", [P, KT * INNER])
        bias_c = sb("bias_c", [P, H, N])
        nb_row = sb("nb_row", [P, H])
        gin_col = sb("gin_col", [P, KT])
        gout_row = sb("gout_row", [P, DIM])
        nk_col = sb("nk_col", [DH, 1])
        nv_col = sb("nv_col", [P, 1])
        eps_col = sb("eps_col", [P, 2])
        pow_col = sb("pow_col", [P, 2])
        x_in = sb("x_in", [P, 2, GB, DIM])
        x_res = sb("x_res", [P, 2, GB, DIM])
        mask_u8 = sb("mask_u8", [P, 2, GB, N], U8)
        mask_add = sb("mask_add", [P, 2, GB, N])
        x_stats = sb("x_stats", [P, GB, 6])
        x_mv = sb("x_mv", [P, GB, 2])
        x_var = sb("x_var", [P, GB])
        x_rstd = sb("x_rstd", [P, GB])
        xn = sb("xn", [P, GB, DIM])
        xt_hi, xt_lo = sb("xt_hi", [P, KT, TOK], F32R), sb("xt_lo", [P, KT, TOK], F32R)
        k_raw = sb("k_raw", [DH, TOK])
        v_raw = sb("v_raw", [P, TOK])
        keys = sb("keys", [P, 2, GB, 2, N], F32R)
        v_hi, v_lo = sb("v_hi", [P, 2, GB, 3 * DH], F32R), sb("v_lo", [P, 2, GB, 3 * DH], F32R)
        q_sb = sb("q_sb", [P, 2, H, TOK], F32R)
        bias_b = sb("bias_b", [P, 2, HC, N])
        s_low = sb("s_low", [P, 2, 2, N])
        logit = sb("logit", [P, 2, HC, N + 1])
        neg_max = sb("neg_max", [P, 2, HC])
        w_exp = sb("w_exp", [P, 2, HC, N + 1])
        w_sum = sb("w_sum", [P, 2, HC])
        w_inv = sb("w_inv", [P, 2, HC])
        w_nrm = sb("w_nrm", [P, 2, HC, N])
        wt_hi, wt_lo = sb("wt_hi", [P, 2, HC, N], F32R), sb("wt_lo", [P, 2, HC, N], F32R)
        o_hi, o_lo = sb("o_hi", [P, 2, 2, N], F32R), sb("o_lo", [P, 2, 2, N], F32R)
        y_stats = sb("y_stats", [P, 2, 6])
        y_mv = sb("y_mv", [P, 2, 2])
        y_var = sb("y_var", [P, 2])
        y_rstd = sb("y_rstd", [P, 2])
        y_shift = sb("y_shift", [P, 2])
        y_nrm = sb("y_nrm", [P, 2, DIM])
        y_out = sb("y_out", [P, 2, DIM])

        ps_s = [psum(f"ps_s{i}", [P, 2, 2, N]) for i in range(2)]
        ps_wt = psum("ps_wt", [P, HC, N])
        ps_pv = psum("ps_pv", [P, 2, N])
        ps_proj = [psum(f"ps_proj{i}", [P, 512]) for i in range(2)]
        ps_o = [psum(f"ps_o{i}", [P, DIM]) for i in range(2)]

        ld_const = sem("ld_const")
        ld_wkv, ld_wq, ld_wo = sem("ld_wkv"), sem("ld_wq"), sem("ld_wo")
        ld_bias = sem("ld_bias")
        ld_x = [sem(f"ld_x{i}") for i in range(2)]
        ld_mask = [sem(f"ld_mask{i}") for i in range(2)]
        x_copied = [sem(f"x_copied{i}") for i in range(2)]
        stored = [sem(f"stored{i}") for i in range(2)]
        ident_zero, ident_made = sem("ident_zero"), sem("ident_made")
        filled = sem("filled")
        waits_taken = sem("waits_taken")
        w_hi_made, w_lo_made = sem("w_hi_made"), sem("w_lo_made")
        bias_shifted, bias_made = sem("bias_shifted"), sem("bias_made")
        mask_made = sem("mask_made")
        x_stat_made, x_mv_made, x_var_made, x_rstd_made = (sem("x_stat_made"), sem("x_mv_made"),
                                                           sem("x_var_made"), sem("x_rstd_made"))
        xn_made = sem("xn_made")
        proj_done = sem("proj_done")
        proj_read = sem("proj_read")
        xt_hi_made = sem("xt_hi_made")
        k_raw_made, v_raw_made = sem("k_raw_made"), sem("v_raw_made")
        k_hi_made, k_lo_made = sem("k_hi_made"), sem("k_lo_made")
        v_hi_made = sem("v_hi_made")
        q_hi_made = sem("q_hi_made")
        s_done, s_low_made, s_read = sem("s_done"), sem("s_low_made"), sem("s_read")
        bias_b_made = sem("bias_b_made")
        exp_made, inv_made, nrm_made = sem("exp_made"), sem("inv_made"), sem("nrm_made")
        wt_done, wt_hi_made, wt_lo_made = sem("wt_done"), sem("wt_hi_made"), sem("wt_lo_made")
        pv_done, o_hi_made, o_lo_made = sem("pv_done"), sem("o_hi_made"), sem("o_lo_made")
        o_done = sem("o_done")
        y_stat_made, y_mv_made, y_var_made, y_rstd_made, y_shift_made = (
            sem("y_stat_made"), sem("y_mv_made"), sem("y_var_made"), sem("y_rstd_made"), sem("y_shift_made"))
        y_nrm_made, y_g_made, y_out_made = sem("y_nrm_made"), sem("y_g_made"), sem("y_out_made")

        CONST_LOADS = 8

        def wait(eng, s, value):
            if isinstance(value, int) and value <= 0:
                return
            eng.wait_ge(s, value)

        def apart(eng):
            eng.sem_inc(waits_taken, 1)

        def run_pairs(eng, body):
            body(0, True, False)
            with eng.Fori(1, PAIRS - 1) as p:
                body(p, False, False)
            body(PAIRS - 1, False, True)

        def steps(last):
            return range(CP + (TAIL if last else 0))

        def live(t, lag, first, last):
            return not (first and t < lag) and t - lag < CP

        def out_batch(p, t, step, first, last):
            back = t // CB - 2
            if t % CB != step or (first and back < 0) or (last and back >= 2 * GB):
                return None
            return 2 * GB * p + back, (t - 2 * CB) % CP

        def front_parts(p, t, first, last):
            if (first and t < 0) or t >= CP:
                return
            for kind, i, ahead in FRONT[t % CG]:
                if first and t < CG and ahead == 0 or last and t // CG + ahead == 2:
                    continue
                yield 2 * p + t // CG + ahead, (t // CG + ahead) % 2, kind, i

        block = ctx.enter_context(nc.Block())

        @block.sync
        def _(sp):
            def copy_x(q, k):
                sp.wait_ge(ld_x[k], 16 * (q + 1))
                apart(sp)
                sp.dma_start(x_res[:, k], x_in[:, k]).then_inc(x_copied[k], 16)

            def reload_x(q, k):
                sp.wait_ge(x_copied[k], 16 * q)
                apart(sp)
                sp.wait_ge(xn_made, GB * (2 * q + k - 1))
                apart(sp)
                sp.wait_ge(mask_made, 2 * q + k - 1)
                apart(sp)
                load_x(q, k)

            def load_x(q, k):
                sp.dma_start(x_in[:, k], x_pairs[q, :, GB * k:GB * (k + 1), :]).then_inc(ld_x[k], 16)
                sp.dma_start(mask_u8[:, k].rearrange("p b n -> p (b n)"),
                             mask_pairs[q, TOK * k:TOK * (k + 1)].partition_broadcast(P)).then_inc(ld_mask[k], 16)

            sp.dma_start(gin_col[:], g_in.rearrange("(k p) -> p k", p=P),
                         allow_slow_non_contiguous=True).then_inc(ld_const, 16)
            load_x(0, 0)
            sp.dma_start(w_raw[:, 0:KT * 2 * DH].rearrange("p (k n) -> p k n", k=KT),
                         wkv.rearrange("(k p) n -> p k n", p=P)).then_inc(ld_wkv, 16)
            load_x(0, 1)
            sp.dma_start(gout_row[:], g_out.partition_broadcast(P)).then_inc(ld_const, 16)
            sp.dma_start(nb_row[:], null_bias.partition_broadcast(P)).then_inc(ld_const, 16)
            sp.dma_start(nk_col[:], null_kv[0].rearrange("(d o) -> d o", o=1)).then_inc(ld_const, 16)
            sp.dma_start(nv_col[0:DH], null_kv[1].rearrange("(d o) -> d o", o=1)).then_inc(ld_const, 16)
            sp.dma_start(nv_col[DH:P], null_kv[1].rearrange("(d o) -> d o", o=1)).then_inc(ld_const, 16)
            sp.dma_start(bias_c[:], attn_bias.rearrange("h i j -> i h j")).then_inc(ld_bias, 16)
            sp.wait_ge(w_lo_made, 1)
            sp.dma_start(w_raw[:].rearrange("p (k n) -> p k n", k=KT),
                         wq.rearrange("(k p) n -> p k n", p=P)).then_inc(ld_wq, 16)
            sp.wait_ge(w_lo_made, 2)
            sp.dma_start(w_raw[:].rearrange("p (k n) -> p k n", k=OT),
                         wo.rearrange("(k p) n -> p k n", p=P)).then_inc(ld_wo, 16)

            for k in range(2):
                copy_x(0, k)
            for k in range(2):
                reload_x(1, k)

            def body(p, copies, loads):
                for k in range(2):
                    for b in range(GB):
                        sp.wait_ge(y_out_made, GB * (2 * p + k) + b + 1)
                        apart(sp)
                        sp.dma_start(out_pairs[p, :, GB * k + b, :], y_out[:, b]).then_inc(stored[b], 16)
                    if copies:
                        copy_x(p + 1, k)
                    if loads:
                        reload_x(p + 2, k)

            with sp.Fori(0, PAIRS - 2) as p:
                body(p, True, True)
            body(PAIRS - 2, True, False)
            body(PAIRS - 1, False, False)
            for b in range(GB):
                sp.wait_ge(stored[b], 16 * GROUPS)

        @block.tensor
        def _(pe):
            def scores(n, g, t):
                b, c, slot = t // CB % GB, t % CB, t // CG
                if b == 0:
                    wait(pe, proj_read, USES * g + USE["q", HC // 2 * (c + 1) - 1] + 1)
                    if c == 0:
                        wait(pe, k_lo_made, g + 1)
                for u in range(2):
                    wait(pe, s_read, 2 * n + u - 1)
                    for i in range(2):
                        h = HC * c + 2 * u + i
                        mm = pe.matmul(ps_s[u][:, i].rearrange("p a n -> p (a n)"), q_sb[:, slot, h, N * b:N * (b + 1)],
                                       keys[:, slot, b].rearrange("p a n -> p (a n)"), start=True, stop=True)
                    mm.then_inc(s_done, 1)

            def weights_t(n, t):
                s = t % 2
                wait(pe, nrm_made, n + 1)
                wait(pe, wt_lo_made, n)
                for i in range(HC):
                    mm = pe.transpose(ps_wt[:, i], w_nrm[:, s, i], ident[:])
                mm.then_inc(wt_done, 1)

            def values(n, g, t):
                b, s, slot = t // CB % GB, t % 2, t // CG % 2
                wait(pe, wt_lo_made, n + 1)
                wait(pe, o_lo_made, n)
                if t % CG == 0:
                    wait(pe, proj_read, USES * g + USE["v", 0] + 1)
                even, odd = slice(DH, 3 * DH), slice(0, 2 * DH)
                todo = [(v, w, par) for v, w in ((v_hi, wt_hi), (v_lo, wt_hi), (v_hi, wt_lo)) for par in range(2)]
                for j, (v, w, par) in enumerate(todo):
                    mm = pe.matmul(ps_pv[:], v[:, slot, b, odd if par else even], w[:, s, par::2],
                                   start=(j == 0), stop=(j == len(todo) - 1))
                mm.then_inc(pv_done, 1)

            def project_out(n, batch, t):
                b, c, s = t // CB % GB, t % CB, t % 2
                wait(pe, o_lo_made, n + 1)
                if c == 0:
                    wait(pe, y_nrm_made, batch - 1)
                todo = [(o, w, i) for i in range(2) for o, w in ((o_hi, wo_hi), (o_hi, wo_lo), (o_lo, wo_hi))]
                for j, (o, w, i) in enumerate(todo):
                    mm = pe.matmul(ps_o[b][:], o[:, s, i], w[:, 2 * c + i],
                                   start=(c == 0 and j == 0), stop=(c == CB - 1 and j == len(todo) - 1))
                mm.then_inc(o_done, 1)

            def project(ps, f, w_hi, w_lo, cols):
                todo = [(k, w, xt) for k in range(KT) for w, xt in ((w_hi, xt_hi), (w_lo, xt_hi), (w_hi, xt_lo))]
                for j, (k, w, xt) in enumerate(todo):
                    mm = pe.matmul(ps[:, 0:TOK], w[:, k, cols], xt[:, k], start=(j == 0), stop=(j == len(todo) - 1))
                return mm

            def front(f, kind, i):
                use = USE[kind, i]
                ps = ps_proj[use % 2]
                wait(pe, proj_read, USES * f + use - 1)
                if kind == "x":
                    if i == 0:
                        wait(pe, xn_made, GB * (f + 1))
                    for j in range(KX * GB):
                        k, b = KX * i + j // GB, j % GB
                        mm = pe.transpose(ps[:, N * j:N * (j + 1)], xn[:, b, P * k:P * (k + 1)], ident[:])
                elif kind == "kv":
                    wait(pe, proj_read, USES * f + XT)
                    mm = project(ps, f, wkv_hi, wkv_lo, slice(0, 2 * DH))
                elif kind == "v":
                    wait(pe, v_raw_made, f + 1)
                    apart(pe)
                    for b in range(GB):
                        mm = pe.transpose(ps[:, DH * b:DH * (b + 1)], v_raw[DH:P, N * b:N * (b + 1)], ident[DH:P, DH:P])
                else:
                    mm = project(ps, f, wq_hi, wq_lo, slice(P * i, P * (i + 1)))
                mm.then_inc(proj_done, 1)

            pe.wait_ge(ident_made, 1)
            for kind, i in USE:
                if kind == "kv":
                    pe.wait_ge(w_lo_made, 1)
                if kind == "q" and i == 0:
                    pe.wait_ge(w_lo_made, 2)
                front(0, kind, i)
            scores(0, 0, 0)

            def body(p, first, last):
                for t in steps(last):
                    n = CP * p + t
                    if live(t, LAG_T, first, last):
                        weights_t(n - LAG_T, t - LAG_T)
                    if first and t == LAG_O:
                        pe.wait_ge(w_lo_made, 3)
                    if live(t, LAG_O, first, last):
                        project_out(n - LAG_O, 2 * GB * p + (t - LAG_O) // CB, (t - LAG_O) % CP)
                    if t + 1 < CP + (not last):
                        scores(n + 1, 2 * p + (t + 1) // CG, (t + 1) % CP)
                    if live(t, LAG_PV, first, last):
                        values(n - LAG_PV, 2 * p + (t - LAG_PV) // CG, (t - LAG_PV) % CP)
                    for f, slot, kind, i in front_parts(p, t, first, last):
                        front(f, kind, i)

            run_pairs(pe, body)

        @block.vector
        def _(dve):
            def logits(n, g, t):
                b, c, s = t // CB % GB, t % CB, t % 2
                wait(dve, bias_b_made, n + 1)
                for u in range(2):
                    wait(dve, s_done, 2 * n + u + 1)
                    wait(dve, s_read, 2 * n + u - 1)
                    nc.vector.tensor_tensor(s_low[:, u], ps_s[u][:, :, 1], bias_b[:, s, 2 * u:2 * u + 2],
                                            ALU.add).then_inc(s_low_made, 1)
                wait(dve, exp_made, n - 1)
                for u in range(2):
                    wait(dve, s_low_made, 2 * n + u + 1)
                    apart(dve)
                    for i in range(2):
                        j = 2 * u + i
                        ins = nc.vector.tensor_tensor_reduce(
                            logit[:, s, j, 0:N], ps_s[u][:, i, 0], s_low[:, u, i], -1.0, 0.0, ALU.add, ALU.min,
                            neg_max[:, s, j:j + 1])
                    ins.then_inc(s_read, 1)

            def inverse(n, t):
                s = t % 2
                wait(dve, exp_made, n + 1)
                wait(dve, nrm_made, n - 1)
                nc.vector.reciprocal(w_inv[:, s], w_sum[:, s]).then_inc(inv_made, 1)

            def weights_lo(n, t):
                s = t % 2
                wait(dve, wt_hi_made, n + 1)
                wait(dve, pv_done, n - 1)
                nc.vector.tensor_tensor(wt_lo[:, s], ps_wt[:], wt_hi[:, s].bitcast(F32),
                                        ALU.subtract).then_inc(wt_lo_made, 1)

            def heads_lo(n, t):
                s = t % 2
                wait(dve, o_hi_made, n + 1)
                wait(dve, o_done, n - 1)
                nc.vector.scalar_tensor_tensor(out=o_lo[:, s], in0=ps_pv[:], scalar=nv_col[:, 0:1],
                                               in1=o_hi[:, s].bitcast(F32), op0=ALU.add,
                                               op1=ALU.subtract).then_inc(o_lo_made, 1)

            def out_stats(batch, t):
                b = t // CB % GB
                wait(dve, o_done, CB * (batch + 1))
                wait(dve, y_mv_made, batch)
                nc.vector.bn_stats(y_stats[:, b], ps_o[b][:]).then_inc(y_stat_made, 1)
                wait(dve, y_stat_made, batch + 1)
                wait(dve, y_shift_made, batch - 1)
                apart(dve)
                nc.vector.bn_aggr(y_mv[:, b], y_stats[:, b]).then_inc(y_mv_made, 1)

            def x_stats_of(f, k):
                wait(dve, ld_x[k], 8 * (f - k) + 16)
                for b in range(GB):
                    wait(dve, x_mv_made, GB * f + b - 1)
                    nc.vector.bn_stats(x_stats[:, b], x_in[:, k, b]).then_inc(x_stat_made, 1)
                wait(dve, x_rstd_made, f)
                wait(dve, xn_made, GB * f)
                for b in range(GB):
                    wait(dve, x_stat_made, GB * f + b + 1)
                    apart(dve)
                    nc.vector.bn_aggr(x_mv[:, b], x_stats[:, b]).then_inc(x_mv_made, 1)

            def x_norm(f, k):
                wait(dve, x_rstd_made, f + 1)
                wait(dve, x_mv_made, GB * (f + 1))
                wait(dve, proj_done, USES * (f - 1) + XT)
                for b in range(GB):
                    nc.vector.tensor_scalar(xn[:, b], x_in[:, k, b], x_mv[:, b, 0:1], x_rstd[:, b:b + 1],
                                            ALU.subtract, ALU.mult).then_inc(xn_made, 1)
                wait(dve, ld_mask[k], 8 * (f - k) + 16)
                wait(dve, bias_b_made, CG * (f - 1))
                nc.vector.tensor_scalar(mask_add[:, k], mask_u8[:, k], MASKED, -MASKED, ALU.mult,
                                        ALU.add).then_inc(mask_made, 1)

            def front(f, slot, kind, i):
                use = USE[kind, i]
                ps = ps_proj[use % 2]
                if kind == "x":
                    wait(dve, xt_hi_made, KT * f + KX * (i + 1))
                    for j in range(KX):
                        k = KX * i + j
                        ins = nc.vector.scalar_tensor_tensor(
                            out=xt_lo[:, k], in0=ps[:, TOK * j:TOK * (j + 1)], scalar=gin_col[:, k:k + 1],
                            in1=xt_hi[:, k].bitcast(F32), op0=ALU.mult, op1=ALU.subtract)
                    ins.then_inc(proj_read, 1)
                elif kind == "kv":
                    wait(dve, proj_done, USES * f + use + 1)
                    wait(dve, k_lo_made, f)
                    wait(dve, k_hi_made, 2 * f)
                    nc.vector.tensor_scalar(k_raw[:], ps[0:DH, 0:TOK], nk_col[:, 0:1], SCALE, ALU.subtract,
                                            ALU.mult).then_inc(k_raw_made, 1)
                    wait(dve, proj_done, USES * (f - 1) + USE["v", 0] + 1)
                    nc.vector.tensor_scalar(v_raw[DH:P, :], ps[DH:P, 0:TOK], nv_col[DH:P, 0:1], None,
                                            ALU.subtract).then_inc(v_raw_made, 1)
                    wait(dve, v_raw_made, f + 1)
                    wait(dve, k_raw_made, f + 1)
                    dve.sem_inc(proj_read, 1)
                elif kind == "v":
                    wait(dve, v_hi_made, f + 1)
                    nc.vector.tensor_tensor(v_lo[:, slot, :, DH:2 * DH],
                                            ps[:, 0:GB * DH].rearrange("p (b d) -> p b d", b=GB),
                                            v_hi[:, slot, :, DH:2 * DH].bitcast(F32), ALU.subtract
                                            ).then_inc(proj_read, 1)
                else:
                    for half in range(2):
                        up, across = slice(DH * half, DH * (half + 1)), slice(DH * (1 - half), DH * (2 - half))
                        wait(dve, q_hi_made, 2 * QT * f + 2 * i + half + 1)
                        ins = nc.vector.tensor_tensor(q_sb[across, slot, 2 * i + half], ps[up, 0:TOK],
                                                      q_sb[up, slot, 2 * i + half].bitcast(F32), ALU.subtract)
                    ins.then_inc(proj_read, 1)

            def keys_lo(f, slot):
                wait(dve, k_hi_made, 2 * f + 2)
                for half in range(2):
                    ins = nc.vector.tensor_tensor(
                        keys[DH * half:DH * (half + 1), slot, :, 1], k_raw[:].rearrange("p (b n) -> p b n", b=GB),
                        keys[0:DH, slot, :, 0].bitcast(F32), ALU.subtract)
                ins.then_inc(k_lo_made, 1)

            for z in (v_hi, v_lo):
                nc.vector.memset(z[:, :, :, 0:DH].bitcast(F32), 0.0)
                nc.vector.memset(z[:, :, :, 2 * DH:3 * DH].bitcast(F32), 0.0)
            nc.vector.memset(eps_col[:], EPS)
            nc.vector.memset(pow_col[:], -0.5)
            nc.vector.memset(logit[:, :, :, N:N + 1], 0.0).then_inc(filled, 1)
            x_stats_of(0, 0)
            x_norm(0, 0)
            dve.wait_ge(ld_wkv, 16)
            dve.wait_ge(w_hi_made, 1)
            nc.vector.tensor_tensor(wkv_lo[:].rearrange("p k n -> p (k n)"), w_raw[:, 0:KT * 2 * DH],
                                    wkv_hi[:].rearrange("p k n -> p (k n)").bitcast(F32),
                                    ALU.subtract).then_inc(w_lo_made, 1)
            dve.wait_ge(ld_const, 16 * 6)
            for i in range(XT):
                front(0, 0, "x", i)
            x_stats_of(1, 1)
            x_norm(1, 1)
            front(0, 0, "kv", 0)
            keys_lo(0, 0)
            dve.wait_ge(ld_bias, 16)
            nc.vector.tensor_tensor(bias_c[:], bias_c[:], nb_row[:].unsqueeze(2).to_broadcast([P, H, N]),
                                    ALU.subtract).then_inc(bias_shifted, 1)
            dve.wait_ge(w_hi_made, 2)
            nc.vector.tensor_tensor(wq_lo[:].rearrange("p k n -> p (k n)"), w_raw[:],
                                    wq_hi[:].rearrange("p k n -> p (k n)").bitcast(F32),
                                    ALU.subtract).then_inc(w_lo_made, 1)
            for kind, i in list(USE)[XT + 1:]:
                front(0, 0, kind, i)
            dve.wait_ge(w_hi_made, 3)
            nc.vector.tensor_tensor(wo_lo[:].rearrange("p k n -> p (k n)"), w_raw[:],
                                    wo_hi[:].rearrange("p k n -> p (k n)").bitcast(F32),
                                    ALU.subtract).then_inc(w_lo_made, 1)

            def body(p, first, last):
                for t in steps(last):
                    n = CP * p + t
                    if t < CP:
                        logits(n, 2 * p + t // CG, t)
                    if live(t, LAG_SUM, first, last):
                        inverse(n - LAG_SUM, t - LAG_SUM)
                    if live(t, LAG_HEADS, first, last):
                        heads_lo(n - LAG_HEADS, t - LAG_HEADS)
                    for f, slot, kind, i in front_parts(p, t - 1, first, last):
                        front(f, slot, kind, i)
                    if live(t, LAG_T, first, last):
                        weights_lo(n - LAG_T, t - LAG_T)
                    if t < CP and t % CG == STEP_K_LO and not (last and t >= CG):
                        keys_lo(2 * p + t // CG + 1, (t // CG + 1) % 2)
                    if done := out_batch(p, t, STEP_OUT_STATS, first, last):
                        out_stats(*done)
                    if not last:
                        if t % CG == STEP_STATS:
                            x_stats_of(2 * p + t // CG + 2, t // CG)
                        if t % CG == STEP_XN:
                            x_norm(2 * p + t // CG + 2, t // CG)

            run_pairs(dve, body)

        @block.scalar
        def _(act):
            def weights_hi(n, t):
                s = t % 2
                wait(act, wt_done, n + 1)
                wait(act, pv_done, n - 1)
                nc.scalar.copy(wt_hi[:, s], ps_wt[:]).then_inc(wt_hi_made, 1)

            def exponentials(n, t):
                s = t % 2
                wait(act, nrm_made, n - 1)
                wait(act, inv_made, n - 1)
                for j in range(HC):
                    if j % 2 == 0:
                        wait(act, s_read, 2 * n + j // 2 + 1)
                    ins = nc.scalar.activation(w_exp[:, s, j], logit[:, s, j], ACT.Exp, bias=neg_max[:, s, j:j + 1],
                                               scale=-1.0, accum_out=w_sum[:, s, j:j + 1])
                ins.then_inc(exp_made, 1)

            def heads_hi(n, t):
                s = t % 2
                wait(act, pv_done, n + 1)
                wait(act, o_done, n - 1)
                nc.scalar.activation(o_hi[:, s], ps_pv[:], ACT.Identity, bias=nv_col[:, 0:1]).then_inc(o_hi_made, 1)

            def out_norm(batch, t):
                b = t // CB % GB
                wait(act, y_shift_made, batch + 1)
                wait(act, y_out_made, batch - 1)
                nc.scalar.activation(y_nrm[:, b], ps_o[b][:], ACT.Identity, bias=y_shift[:, b:b + 1],
                                     scale=y_rstd[:, b:b + 1]).then_inc(y_nrm_made, 1)

            def front(f, slot, kind, i):
                use = USE[kind, i]
                ps = ps_proj[use % 2]
                if kind == "x":
                    wait(act, proj_done, USES * f + use + 1)
                    for j in range(KX):
                        k = KX * i + j
                        nc.scalar.activation(xt_hi[:, k], ps[:, TOK * j:TOK * (j + 1)], ACT.Copy,
                                             scale=gin_col[:, k:k + 1]).then_inc(xt_hi_made, 1)
                elif kind == "kv":
                    wait(act, k_raw_made, f + 1)
                    for half in range(2):
                        nc.scalar.copy(keys[DH * half:DH * (half + 1), slot, :, 0],
                                       k_raw[:].rearrange("p (b n) -> p b n", b=GB)).then_inc(k_hi_made, 1)
                elif kind == "v":
                    wait(act, proj_done, USES * f + use + 1)
                    nc.scalar.copy(v_hi[:, slot, :, DH:2 * DH],
                                   ps[:, 0:GB * DH].rearrange("p (b d) -> p b d", b=GB)).then_inc(v_hi_made, 1)
                else:
                    wait(act, proj_done, USES * f + use + 1)
                    for half in range(2):
                        up = slice(DH * half, DH * (half + 1))
                        nc.scalar.copy(q_sb[up, slot, 2 * i + half], ps[up, 0:TOK]).then_inc(q_hi_made, 1)

            act.wait_ge(ld_wkv, 16)
            nc.scalar.copy(wkv_hi[:].rearrange("p k n -> p (k n)"), w_raw[:, 0:KT * 2 * DH]).then_inc(w_hi_made, 1)
            act.wait_ge(ld_const, 16 * 6)
            for i in range(XT):
                front(0, 0, "x", i)
            front(0, 0, "kv", 0)
            act.wait_ge(ld_wq, 16)
            nc.scalar.copy(wq_hi[:].rearrange("p k n -> p (k n)"), w_raw[:]).then_inc(w_hi_made, 1)
            act.wait_ge(filled, 1)
            for kind, i in list(USE)[XT + 1:]:
                front(0, 0, kind, i)
            act.wait_ge(ld_wo, 16)
            nc.scalar.copy(wo_hi[:].rearrange("p k n -> p (k n)"), w_raw[:]).then_inc(w_hi_made, 1)

            def body(p, first, last):
                for t in steps(last):
                    n = CP * p + t
                    if live(t, LAG_HEADS, first, last):
                        heads_hi(n - LAG_HEADS, t - LAG_HEADS)
                    for f, slot, kind, i in front_parts(p, t - 1, first, last):
                        front(f, slot, kind, i)
                    if live(t, LAG_T, first, last):
                        weights_hi(n - LAG_T, t - LAG_T)
                    if done := out_batch(p, t, STEP_OUT_NORM, first, last):
                        out_norm(*done)
                    if t < CP:
                        exponentials(n, t)

            run_pairs(act, body)

        @block.gpsimd
        def _(pool):
            def masked_bias(n, g, t):
                slot, b, c, s = t // CG % 2, t // CB % GB, t % CB, t % 2
                if t % CG == 0:
                    wait(pool, mask_made, g + 1)
                wait(pool, s_low_made, 2 * (n - 1))
                nc.gpsimd.tensor_tensor(bias_b[:, s], bias_c[:, HC * c:HC * (c + 1)],
                                        mask_add[:, slot, b].unsqueeze(1).to_broadcast([P, HC, N]),
                                        ALU.add).then_inc(bias_b_made, 1)

            def normalize(n, t):
                s = t % 2
                wait(pool, inv_made, n + 1)
                wait(pool, wt_done, n - 1)
                nc.gpsimd.tensor_tensor(w_nrm[:, s], w_exp[:, s, :, 0:N],
                                        w_inv[:, s].unsqueeze(2).to_broadcast([P, HC, N]),
                                        ALU.mult).then_inc(nrm_made, 1)

            def x_rstd_of(f):
                wait(pool, x_mv_made, GB * (f + 1))
                wait(pool, x_rstd_made, f)
                nc.gpsimd.tensor_tensor(x_var[:], x_mv[:, :, 1], eps_col[:], ALU.add).then_inc(x_var_made, 1)
                wait(pool, x_var_made, f + 1)
                wait(pool, xn_made, GB * f)
                nc.gpsimd.tensor_tensor(x_rstd[:], x_var[:], pow_col[:], ALU.pow).then_inc(x_rstd_made, 1)

            def y_scale(batch, t):
                b = t // CB % GB
                c = slice(b, b + 1)
                wait(pool, y_mv_made, batch + 1)
                wait(pool, y_nrm_made, batch - 1)
                nc.gpsimd.tensor_tensor(y_var[:, c], y_mv[:, b, 1:2], eps_col[:, 0:1], ALU.add).then_inc(y_var_made, 1)
                wait(pool, y_var_made, batch + 1)
                nc.gpsimd.tensor_tensor(y_rstd[:, c], y_var[:, c], pow_col[:, 0:1], ALU.pow).then_inc(y_rstd_made, 1)
                wait(pool, y_rstd_made, batch + 1)
                apart(pool)
                nc.gpsimd.tensor_scalar(y_shift[:, c], y_mv[:, b, 0:1], -1.0, y_rstd[:, c], ALU.mult,
                                        ALU.mult).then_inc(y_shift_made, 1)

            def residual(batch, p, t):
                slot, b = t // CG % 2, t // CB % GB
                wait(pool, y_nrm_made, batch + 1)
                nc.gpsimd.tensor_tensor(y_nrm[:, b], y_nrm[:, b], gout_row[:], ALU.mult).then_inc(y_g_made, 1)
                wait(pool, y_g_made, batch + 1)
                if b == 0:
                    wait(pool, x_copied[slot], 16 * (p + 1))
                wait(pool, stored[b], stored_before(batch, b))
                nc.gpsimd.tensor_tensor(y_out[:, b], y_nrm[:, b], x_res[:, slot, b], ALU.add).then_inc(y_out_made, 1)

            def stored_before(batch, b):
                return 8 * (batch - b)

            nc.gpsimd.memset(ident[:], 0.0).then_inc(ident_zero, 1)
            pool.wait_ge(ident_zero, 1)
            nc.gpsimd.affine_select(out=ident[:], in_=ident[:], compare_op=ALU.not_equal, fill=1.0, base=0,
                                    pattern=[[-1, P]], channel_multiplier=1).then_inc(ident_made, 1)
            pool.wait_ge(filled, 1)
            x_rstd_of(0)
            x_rstd_of(1)
            pool.wait_ge(bias_shifted, 1)
            nc.gpsimd.affine_select(out=bias_c[:], in_=bias_c[:], compare_op=ALU.is_ge, fill=-MASKED, base=0,
                                    pattern=[[0, H], [-1, N]], channel_multiplier=1).then_inc(bias_made, 1)
            pool.wait_ge(bias_made, 1)
            masked_bias(0, 0, 0)

            def body(p, first, last):
                for t in steps(last):
                    n = CP * p + t
                    if live(t, LAG_SUM, first, last):
                        normalize(n - LAG_SUM, t - LAG_SUM)
                    if t < CP and not (last and t == CP - 1):
                        masked_bias(n + 1, 2 * p + (t + 1) // CG, (t + 1) % CP)
                    if not last and t % CG == STEP_STATS:
                        x_rstd_of(2 * p + t // CG + 2)
                    if done := out_batch(p, t, STEP_OUT_STATS, first, last):
                        y_scale(*done)
                    if done := out_batch(p, t, STEP_OUT_ADD, first, last):
                        residual(done[0], p + (t // CB - 2) // (2 * GB), done[1])

            run_pairs(pool, body)


_INS = ["x", "fside_16xSxS_0", "cond_64", "mask_BxS_bk0", "L0_cond_g_in", "L0_cond_null_attn_bias", "L0_cond_Wq",
        "L0_cond_Wkv", "L0_cond_Wo", "L0_cond_g_out"]


def kernel(**inputs):
    import numpy as _np
    import concourse.bacc as _bacc
    from concourse import mybir as _mybir
    from concourse.bass_utils import run_bass_kernel_spmd as _run

    nc = _bacc.Bacc("TRN2", target_bir_lowering=False, num_devices=1)
    arrays, args = {}, []
    for name in _INS:
        a = _np.ascontiguousarray(inputs[name])
        arrays[f"in_{name}_dram"] = a
        args.append(nc.dram_tensor(f"in_{name}_dram", a.shape, _mybir.dt.from_np(a.dtype), kind="ExternalInput").ap())
    out = nc.dram_tensor("out_dram", (B, N, DIM), F32, kind="ExternalOutput").ap()
    attention_block(nc, *args, out)
    r = _run(nc, [arrays], core_ids=[0])
    return r.results[0]["out_dram"]
```

```python
from contextlib import ExitStack

import concourse.bass as bass
from concourse import mybir

F32 = mybir.dt.float32
F32R = mybir.dt.float32r
U8 = mybir.dt.uint8
ALU = mybir.AluOpType
ACT = mybir.ActivationFunctionType

P = 128
B, N, DIM = 64, 128, 512
H, DH = 16, 64
INNER = H * DH
EPS = 1e-5
SCALE = DH ** -0.5
MASKED = 1e38

KT = DIM // P
WP = 4
KX = 2
XT = KT // KX
OT = INNER // P
GB = 2
TOK = GB * N
GROUPS = B // GB
HC = 4
HALF = N // 2
BOT, TOP = 2 * N, 2 * HALF
BLOCKS = (BOT + TOP) // N
CB = H // HC
CG = GB * CB
PAIRS = GROUPS // 2
CP = 2 * CG
QT = INNER // P
LAG_SUM, LAG_T, LAG_PV, LAG_HEADS, LAG_O = 1, 2, 3, 4, 6

FRONT = {
    0: [("q", 7, 0)],
    1: [("x", 0, 1), ("x", 1, 1)],
    2: [("kv", 0, 1)],
    3: [("q", 0, 1), ("q", 1, 1)],
    4: [("v", 0, 1)],
    5: [("q", 2, 1), ("q", 3, 1)],
    6: [("q", 4, 1)],
    7: [("q", 5, 1), ("q", 6, 1)],
}
FRONT_FIRST = {
    0: [("q", 4, 0), ("q", 5, 0)],
    1: [("q", 6, 0), ("q", 7, 0)],
    2: [("x", 0, 1), ("x", 1, 1)],
    3: [("kv", 0, 1)],
    4: [("q", 0, 1), ("q", 1, 1)],
    5: [("v", 0, 1), ("q", 2, 1)],
    6: [("q", 3, 1), ("q", 4, 1)],
    7: [("q", 5, 1), ("q", 6, 1)],
}
STEP_K_LO = 5
USE = {part[:2]: j for j, part in enumerate(sorted((part for parts in FRONT.values() for part in parts),
                                                   key=lambda part: -part[2]))}
USES = len(USE)
READ = {part: j for j, part in enumerate(part for part in USE if part[0] != "kv")}
READS = len(READ)
PROLOGUE = list(USE)[:USE["q", 4]]
STEP_STATS, STEP_XN = 4, 6
STEP_MASK = CG - 1
STEP_OUT_STATS, STEP_OUT_NORM, STEP_OUT_ADD = 1, 3, 4
TAIL = CB + STEP_OUT_ADD + 1


def attention_block(nc, x, attn_bias, null_kv, mask, g_in, null_bias, wq, wkv, wo, g_out, out):
    x_pairs = x.rearrange("(q r) p d -> q p r d", r=2 * GB)
    out_pairs = out.rearrange("(q r) p d -> q p r d", r=2 * GB)
    mask_pairs = mask.rearrange("(q r) n -> q (r n)", r=2 * GB)

    with ExitStack() as ctx:
        def sb(name, shape, dt=F32):
            return ctx.enter_context(nc.sbuf_tensor(name, shape, dt))

        def psum(name, shape):
            return ctx.enter_context(nc.psum_tensor(name, shape, F32))

        def sem(name):
            return ctx.enter_context(nc.semaphore(name))

        small = sb("small", [P, 64])
        columns = iter(range(64))

        def cols(width, rows=P):
            first = [next(columns) for _ in range(width)][0]
            return small[0:rows, first:first + width]

        ident = sb("ident", [P, P])
        wq_hi, wq_lo = sb("wq_hi", [P, KT, INNER], F32R), sb("wq_lo", [P, KT, INNER], F32R)
        wkv_hi, wkv_lo = sb("wkv_hi", [P, KT, 2 * DH], F32R), sb("wkv_lo", [P, KT, 2 * DH], F32R)
        wo_hi, wo_lo = sb("wo_hi", [P, OT, DIM], F32R), sb("wo_lo", [P, OT, DIM], F32R)
        w_raw = sb("w_raw", [P, WP, KT * INNER // WP])
        bias_c = sb("bias_c", [P, CB, BOT + TOP])
        nb_row = sb("nb_row", [P, CB, 2])
        gin_col = cols(KT)
        gout_row = sb("gout_row", [P, DIM])
        nk_col = cols(1, rows=DH)
        k_shift = cols(1, rows=DH)
        nv_col = cols(1)
        v_shift = cols(1)
        minus_one = cols(2)
        eps_col = cols(2)
        pow_col = cols(2)
        x_in = sb("x_in", [P, GB, DIM])
        mask_u8 = sb("mask_u8", [P, 2, GB, N], U8)
        mask_add = sb("mask_add", [P, 2, GB, N])
        x_stats = sb("x_stats", [P, GB, 6])
        x_mv = sb("x_mv", [P, GB, 2])
        x_var = cols(GB)
        x_rstd = cols(GB)
        x_mr = cols(GB)
        x_shift = cols(GB)
        xn = sb("xn", [P, GB, DIM])
        xt_hi, xt_lo = sb("xt_hi", [P, KT, TOK], F32R), sb("xt_lo", [P, KT, TOK], F32R)
        k_raw = sb("k_raw", [P, TOK])
        v_raw = sb("v_raw", [P, HALF + TOK])
        keys = sb("keys", [P, 2, GB, 2, N], F32R)
        v_hi, v_lo = sb("v_hi", [P, 2, GB, 3 * DH], F32R), sb("v_lo", [P, 2, GB, 3 * DH], F32R)
        vd_hi, vd_lo = sb("vd_hi", [P, 2, GB, 2 * DH], F32R), sb("vd_lo", [P, 2, GB, 2 * DH], F32R)
        q_sb = sb("q_sb", [P, 2, CB, 2, 2 * GB, 2, HALF], F32R)
        bias_b = sb("bias_b", [P, 2, BOT + TOP])
        s_low = sb("s_low", [P, BOT + TOP])
        logit_bot, logit_top = sb("logit_bot", [P, 2, 2, N + 1]), sb("logit_top", [P, 2, 2, HALF + 1])
        neg_max = sb("neg_max", [P, 2, HC])
        exp_bot, exp_top = sb("exp_bot", [P, 2, 2, N + 1]), sb("exp_top", [P, 2, 2, HALF + 1])
        w_sum = sb("w_sum", [P, 2, HC])
        w_inv = sb("w_inv", [P, 2, HC])
        w_nrm = sb("w_nrm", [P, 2, BOT + TOP])
        wt_hi, wt_lo = sb("wt_hi", [P, 4, BLOCKS, N], F32R), sb("wt_lo", [P, 4, BLOCKS, N], F32R)
        o_hi, o_lo = sb("o_hi", [P, 2, HC, N], F32R), sb("o_lo", [P, 2, HC, N], F32R)
        y_stats = sb("y_stats", [P, 2, 6])
        y_mv = sb("y_mv", [P, 2, 2])
        y_var = cols(2)
        y_rstd = cols(2)
        y_shift = cols(2)
        y_nrm = sb("y_nrm", [P, 2, DIM])
        y_out = sb("y_out", [P, 2, DIM])
        x_res = sb("x_res", [P, 2, DIM])

        ps_s = psum("ps_s", [P, HC, 2, N])
        ps_wt = psum("ps_wt", [P, BLOCKS, N])
        ps_pv = psum("ps_pv", [P, HC, N])
        ps_proj = [psum(f"ps_proj{i}", [P, 512]) for i in range(2)]
        ps_o = [psum(f"ps_o{i}", [P, DIM]) for i in range(2)]

        ld_cols, ld_rows = sem("ld_cols"), sem("ld_rows")
        ld_wkv = sem("ld_wkv")
        ld_wq, ld_wo = [sem(f"ld_wq{i}") for i in range(WP)], [sem(f"ld_wo{i}") for i in range(WP)]
        ld_bias = sem("ld_bias")
        ld_x = sem("ld_x")
        ld_res = [sem(f"ld_res{i}") for i in range(2)]
        ld_mask = [sem(f"ld_mask{i}") for i in range(2)]
        stored = [sem(f"stored{i}") for i in range(2)]
        ident_zero, ident_made = sem("ident_zero"), sem("ident_made")
        filled = sem("filled")
        waits_taken = sem("waits_taken")
        wkv_hi_made, wkv_lo_made = sem("wkv_hi_made"), sem("wkv_lo_made")
        wq_hi_made, wq_lo_made, wo_hi_made = sem("wq_hi_made"), sem("wq_lo_made"), sem("wo_hi_made")
        wo_lo_by_dve, wo_lo_by_pool = sem("wo_lo_by_dve"), sem("wo_lo_by_pool")
        shifts_made = sem("shifts_made")
        bias_shifted, bias_made = sem("bias_shifted"), sem("bias_made")
        mask_made = sem("mask_made")
        x_stat_made, x_mv_made, x_var_made = sem("x_stat_made"), sem("x_mv_made"), sem("x_var_made")
        x_rstd_made, x_mr_made, x_shift_made = sem("x_rstd_made"), sem("x_mr_made"), sem("x_shift_made")
        xn_made = sem("xn_made")
        proj_done = sem("proj_done")
        proj_read = sem("proj_read")
        xt_hi_made = sem("xt_hi_made")
        k_raw_made, v_raw_made = sem("k_raw_made"), sem("v_raw_made")
        k_hi_made, k_lo_made = sem("k_hi_made"), sem("k_lo_made")
        v_hi_made = sem("v_hi_made")
        q_hi_made = sem("q_hi_made")
        s_done, s_low_made, s_read = sem("s_done"), sem("s_low_made"), sem("s_read")
        bias_b_made = sem("bias_b_made")
        exp_made, inv_made, nrm_made = sem("exp_made"), sem("inv_made"), sem("nrm_made")
        wt_done, wt_hi_made, wt_lo_made = sem("wt_done"), sem("wt_hi_made"), sem("wt_lo_made")
        pv_done, o_hi_made, o_lo_made = sem("pv_done"), sem("o_hi_made"), sem("o_lo_made")
        o_done = sem("o_done")
        y_stat_made, y_mv_made, y_var_made, y_rstd_made, y_shift_made = (
            sem("y_stat_made"), sem("y_mv_made"), sem("y_var_made"), sem("y_rstd_made"), sem("y_shift_made"))
        y_nrm_made, y_g_made, y_out_made = sem("y_nrm_made"), sem("y_g_made"), sem("y_out_made")

        COL_LOADS, ROW_LOADS, BIAS_LOADS = 4, 3, 8
        wkv_raw = y_nrm[:, 0]

        def wq_piece(w, i):
            return w[:, :, INNER // WP * i:INNER // WP * (i + 1)]

        def wo_piece(w, i):
            return w[:, OT // WP * i:OT // WP * (i + 1)]

        def raw_piece(i, k):
            return w_raw[:, i].rearrange("p (k n) -> p k n", k=k)

        def wait(eng, s, value):
            if isinstance(value, int) and value <= 0:
                return
            eng.wait_ge(s, value)

        def apart(eng):
            eng.sem_inc(waits_taken, 1)

        def run_pairs(eng, body):
            body(0, True, False)
            with eng.Fori(1, PAIRS - 1) as p:
                body(p, False, False)
            body(PAIRS - 1, False, True)

        def bot_top(row):
            return row[:, 0:BOT].rearrange("p (e n) -> p e n", e=2), row[:, BOT:].rearrange("p (e n) -> p e n", e=2)

        def copies_of_v(ps, v_hi, v_lo, vd_hi, vd_lo, slot):
            once, again = (ps[:, GB * DH * j:GB * DH * (j + 1)].rearrange("p (b d) -> p b d", b=GB) for j in range(2))
            yield once, v_hi[:, slot, :, DH:2 * DH], v_lo[:, slot, :, DH:2 * DH]
            yield once[0:DH], vd_hi[0:DH, slot, :, 0:DH], vd_lo[0:DH, slot, :, 0:DH]
            yield again[DH:P], vd_hi[DH:P, slot, :, DH:2 * DH], vd_lo[DH:P, slot, :, DH:2 * DH]

        def q_place(up, slot, h):
            return q_sb[up, slot, h // HC, h % 2, :, h // 2 % 2]

        def pair(p, t):
            return CP // 2 * p + t // 2

        def steps(last):
            return range(CP + (TAIL if last else 0))

        def live(t, lag, first, last):
            return not (first and t < lag) and t - lag < CP

        def out_batch(p, t, step, first, last):
            back = (t - step) // CB - 2
            if (t - step) % CB or (first and back < 0) or (last and back >= 2 * GB):
                return None
            return 2 * GB * p + back, back

        def front_parts(p, t, first, last):
            if (first and t < 0) or t >= CP:
                return
            for kind, i, ahead in FRONT_FIRST[t] if first and t < CG else FRONT[t % CG]:
                if last and t // CG + ahead == 2:
                    continue
                yield 2 * p + t // CG + ahead, (t // CG + ahead) % 2, kind, i

        block = ctx.enter_context(nc.Block())

        @block.sync
        def _(sp):
            def load_x(q, k):
                sp.dma_start(x_in[:], x_pairs[q, :, GB * k:GB * (k + 1), :]).then_inc(ld_x, 16)

            def load_mask(q, k):
                sp.dma_start(mask_u8[:, k].rearrange("p b n -> p (b n)"),
                             mask_pairs[q, TOK * k:TOK * (k + 1)].partition_broadcast(P)).then_inc(ld_mask[k], 16)

            def load_x_and_mask(q, k):
                sp.wait_ge(xn_made, GB * (2 * q + k))
                apart(sp)
                sp.wait_ge(mask_made, 2 * q + k - 1)
                apart(sp)
                load_x(q, k)
                load_mask(q, k)

            def load_res(p, k, b):
                sp.dma_start(x_res[:, b], x_pairs[p, :, GB * k + b, :]).then_inc(ld_res[b], 16)

            load_x(0, 0)
            load_mask(0, 0)
            sp.dma_start(gin_col[:], g_in.rearrange("(k p) -> p k", p=P),
                         allow_slow_non_contiguous=True).then_inc(ld_cols, 16)
            sp.dma_start(nk_col[:], null_kv[0].rearrange("(d o) -> d o", o=1)).then_inc(ld_cols, 16)
            for half in range(2):
                sp.dma_start(nv_col[DH * half:DH * (half + 1)],
                             null_kv[1].rearrange("(d o) -> d o", o=1)).then_inc(ld_cols, 16)
            sp.dma_start(wkv_raw.rearrange("p (k n) -> p k n", k=KT),
                         wkv.rearrange("(k p) n -> p k n", p=P)).then_inc(ld_wkv, 16)
            for i in range(WP):
                sp.dma_start(raw_piece(i, KT), wq_piece(wq.rearrange("(k p) n -> p k n", p=P), i)).then_inc(ld_wq[i], 16)
                if i == 1:
                    null_by_head = null_bias.rearrange("(c u e) -> u c e", u=2, e=2)
                    for u in range(2):
                        up = slice(HALF * u, HALF * (u + 1))
                        sp.dma_start(nb_row[up], null_by_head[u].partition_broadcast(HALF),
                                     allow_slow_non_contiguous=True).then_inc(ld_rows, 16)
                    sp.dma_start(gout_row[:], g_out.partition_broadcast(P)).then_inc(ld_rows, 16)
                    by_head = attn_bias.rearrange("(c u e) i j -> u e i c j", u=2, e=2)
                    for u in range(2):
                        up = slice(HALF * u, HALF * (u + 1))
                        for e in range(2):
                            sp.dma_start(bias_c[up, :, N * e:N * (e + 1)], by_head[u, e, HALF:N]).then_inc(ld_bias, 16)
                            sp.dma_start(bias_c[up, :, BOT + HALF * e:BOT + HALF * (e + 1)],
                                         by_head[u, e, 0:HALF, :, 0:HALF]).then_inc(ld_bias, 16)
                    sp.wait_ge(xn_made, GB)
                    load_x(0, 1)
                    load_mask(0, 1)
            for i in range(WP):
                sp.wait_ge(wq_lo_made, i + 1)
                sp.dma_start(raw_piece(i, OT // WP),
                             wo_piece(wo.rearrange("(k p) n -> p k n", p=P), i)).then_inc(ld_wo[i], 16)
            for b in range(GB):
                load_res(0, 0, b)
            for k in range(2):
                load_x_and_mask(1, k)

            def body(p, loads, last):
                for k in range(2):
                    for b in range(GB):
                        sp.wait_ge(y_out_made, GB * (2 * p + k) + b + 1)
                        apart(sp)
                        sp.dma_start(out_pairs[p, :, GB * k + b, :], y_out[:, b]).then_inc(stored[b], 16)
                        if k == 0:
                            load_res(p, 1, b)
                        elif not last:
                            load_res(p + 1, 0, b)
                        if loads and b == 0:
                            load_x_and_mask(p + 2, k)

            with sp.Fori(0, PAIRS - 2) as p:
                body(p, True, False)
            body(PAIRS - 2, False, False)
            body(PAIRS - 1, False, True)
            for b in range(GB):
                sp.wait_ge(stored[b], 16 * GROUPS)

        @block.tensor
        def _(pe):
            def scores(n, g, t):
                b, c, slot = t // CB % GB, t % CB, t // CG
                if b == 0:
                    wait(pe, proj_read, READS * g + READ["q", HC // 2 * (c + 1) - 1] + 1)
                    if c == 0:
                        wait(pe, k_lo_made, g + 1)
                for late in (1, 0):
                    wait(pe, s_read, 2 * n - late)
                    for e in range(2):
                        mm = pe.matmul(ps_s[:, 2 * (1 - late) + e].rearrange("p a n -> p (a n)"),
                                       q_sb[:, slot, c, e, 2 * b + late].rearrange("p u n -> p (u n)"),
                                       keys[:, slot, b].rearrange("p a n -> p (a n)"), start=True, stop=True)
                    mm.then_inc(s_done, 1)

            def weights_t(n, t):
                s = t % 2
                wait(pe, nrm_made, n + 1)
                wait(pe, wt_lo_made, n)
                for i in range(BLOCKS):
                    mm = pe.transpose(ps_wt[:, i], w_nrm[:, s, N * i:N * (i + 1)], ident[:])
                mm.then_inc(wt_done, 1)

            def values(n, u, g, t):
                b, s, slot = t // CB % GB, t % 4 - 1, t // CG % 2
                wait(pe, wt_lo_made, n + 1)
                wait(pe, o_lo_made, u)
                if t % CG == 1:
                    wait(pe, proj_read, READS * g + READ["v", 0] + 1)
                parts = ((v_hi, vd_hi, wt_hi), (v_lo, vd_lo, wt_hi), (v_hi, vd_hi, wt_lo))
                todo = [(v[:, slot, b, DH * (1 - e):DH * (3 - e)], w[:, s:s + 2, e]) for v, _, w in parts for e in range(2)]
                for j, (v, w) in enumerate(todo):
                    pe.matmul(ps_pv[:, :, HALF:N], v, w, start=(j == 0), stop=(j == len(todo) - 1))
                for j, (_, v, w) in enumerate(parts):
                    mm = pe.matmul(ps_pv[:, :, 0:HALF], v[:, slot, b], w[:, s:s + 2, 2],
                                   start=(j == 0), stop=(j == len(parts) - 1))
                mm.then_inc(pv_done, 1)

            def project_out(u, batch, t):
                b, c, s, h = t // CB % GB, t % CB, t // 2 % 2, 2 * (t % 2)
                wait(pe, o_lo_made, u + 1)
                if c == 0:
                    wait(pe, y_nrm_made, batch - 1)
                todo = [(o, w, i) for i in range(2) for o, w in ((o_hi, wo_hi), (o_hi, wo_lo), (o_lo, wo_hi))]
                for j, (o, w, i) in enumerate(todo):
                    mm = pe.matmul(ps_o[b][:], o[:, s, h + i], w[:, 2 * c + i],
                                   start=(c == 0 and j == 0), stop=(c == CB - 1 and j == len(todo) - 1))
                mm.then_inc(o_done, 1)

            def project(ps, f, w_hi, w_lo, cols):
                todo = [(k, w, xt) for k in range(KT) for w, xt in ((w_hi, xt_hi), (w_lo, xt_hi), (w_hi, xt_lo))]
                for j, (k, w, xt) in enumerate(todo):
                    mm = pe.matmul(ps[:, 0:TOK], w[:, k, cols], xt[:, k], start=(j == 0), stop=(j == len(todo) - 1))
                return mm

            def front(f, kind, i):
                use = USE[kind, i]
                ps = ps_proj[use % 2]
                before, part = f + (use - 2) // USES, list(USE)[(use - 2) % USES]
                if part[0] == "kv":
                    wait(pe, v_raw_made, before + 1)
                else:
                    wait(pe, proj_read, READS * before + READ[part] + 1)
                if kind == "x":
                    if i == 0:
                        wait(pe, xn_made, GB * (f + 1))
                    for j in range(KX * GB):
                        k, b = KX * i + j // GB, j % GB
                        mm = pe.transpose(ps[:, N * j:N * (j + 1)], xn[:, b, P * k:P * (k + 1)], ident[:])
                elif kind == "kv":
                    wait(pe, proj_read, READS * f + XT)
                    mm = project(ps, f, wkv_hi, wkv_lo, slice(0, 2 * DH))
                elif kind == "v":
                    wait(pe, v_raw_made, f + 1)
                    apart(pe)
                    for j in range(2 * GB):
                        keys_from = (HALF if j < GB else 0) + N * (j % GB)
                        mm = pe.transpose(ps[:, DH * j:DH * (j + 1)], v_raw[DH:P, keys_from:keys_from + N],
                                          ident[DH:P, DH:P])
                else:
                    if isinstance(f, int) and f == 0:
                        wait(pe, wq_lo_made, i * WP // QT + 1)
                    mm = project(ps, f, wq_hi, wq_lo, slice(P * i, P * (i + 1)))
                mm.then_inc(proj_done, 1)

            pe.wait_ge(ident_made, 1)
            for kind, i in PROLOGUE:
                if kind == "kv":
                    pe.wait_ge(wkv_lo_made, 1)
                front(0, kind, i)
            scores(0, 0, 0)

            def body(p, first, last):
                for t in steps(last):
                    n = CP * p + t
                    if live(t, LAG_T, first, last):
                        weights_t(n - LAG_T, t - LAG_T)
                    if first and t == LAG_O:
                        pe.wait_ge(wo_lo_by_dve, WP // 2)
                        pe.wait_ge(wo_lo_by_pool, WP // 2)
                    if live(t, LAG_O, first, last):
                        project_out(pair(p, t - LAG_O), 2 * GB * p + (t - LAG_O) // CB, (t - LAG_O) % CP)
                    early = first and t < 3
                    if early:
                        for f, slot, kind, i in front_parts(p, t, first, last):
                            front(f, kind, i)
                    if t + 1 < CP + (not last):
                        scores(n + 1, 2 * p + (t + 1) // CG, (t + 1) % CP)
                    if live(t, LAG_PV, first, last) and (t - LAG_PV) % 2:
                        values(n - LAG_PV, pair(p, t - LAG_PV), 2 * p + (t - LAG_PV) // CG, (t - LAG_PV) % CP)
                    if not early:
                        for f, slot, kind, i in front_parts(p, t, first, last):
                            front(f, kind, i)

            run_pairs(pe, body)

        @block.vector
        def _(dve):
            def scores_low(n, t):
                s = t % 2
                wait(dve, bias_b_made, n + 1)
                wait(dve, s_done, 2 * n + 2)
                wait(dve, s_read, 2 * n)
                for i, (out_, bias) in enumerate(zip(bot_top(s_low), bot_top(bias_b[:, s]))):
                    nc.vector.tensor_tensor(out_, ps_s[:, 2 * i:2 * i + 2, 1, 0:out_.shape[2]], bias,
                                            ALU.add).then_inc(s_low_made, 1)

            def logits(n, t):
                s = t % 2
                wait(dve, exp_made, n - 1)
                for i, (low, out_) in enumerate(zip(bot_top(s_low), (logit_bot[:, s], logit_top[:, s]))):
                    wait(dve, s_low_made, 2 * n + 1 + i)
                    apart(dve)
                    keys_ = low.shape[2]
                    for e in range(2):
                        ins = nc.vector.tensor_tensor_reduce(
                            out_[:, e, 0:keys_], ps_s[:, 2 * i + e, 0, 0:keys_], low[:, e], -1.0, 0.0, ALU.add, ALU.min,
                            neg_max[:, s, 2 * i + e:2 * i + e + 1])
                    ins.then_inc(s_read, 1)

            def inverse(n, t):
                s = t % 2
                wait(dve, exp_made, n + 1)
                wait(dve, nrm_made, n - 1)
                nc.vector.reciprocal(w_inv[:, s], w_sum[:, s]).then_inc(inv_made, 1)

            def weights_lo(n, u, t):
                s = t % 4
                wait(dve, wt_hi_made, n + 1)
                wait(dve, pv_done, u - 1)
                nc.vector.tensor_tensor(wt_lo[:, s], ps_wt[:], wt_hi[:, s].bitcast(F32),
                                        ALU.subtract).then_inc(wt_lo_made, 1)

            def heads_lo(u, t):
                s = t // 2 % 2
                wait(dve, o_hi_made, u + 1)
                wait(dve, o_done, 2 * u - 2)
                nc.vector.scalar_tensor_tensor(out=o_lo[:, s], in0=ps_pv[:], scalar=nv_col[:, 0:1],
                                               in1=o_hi[:, s].bitcast(F32), op0=ALU.add,
                                               op1=ALU.subtract).then_inc(o_lo_made, 1)

            def out_stats(batch, back):
                b = back % GB
                wait(dve, o_done, CB * (batch + 1))
                wait(dve, y_mv_made, batch)
                nc.vector.bn_stats(y_stats[:, b], ps_o[b][:]).then_inc(y_stat_made, 1)

            def out_mean_var(batch, back):
                b = back % GB
                wait(dve, y_stat_made, batch + 1)
                wait(dve, y_shift_made, batch - 1)
                apart(dve)
                nc.vector.bn_aggr(y_mv[:, b], y_stats[:, b]).then_inc(y_mv_made, 1)

            def x_stats_of(f):
                wait(dve, ld_x, 16 * (f + 1))
                for b in range(GB):
                    wait(dve, x_mv_made, GB * f + b - 1)
                    nc.vector.bn_stats(x_stats[:, b], x_in[:, b]).then_inc(x_stat_made, 1)

            def x_mean_var_of(f):
                wait(dve, x_shift_made, f)
                for b in range(GB):
                    wait(dve, x_stat_made, GB * f + b + 1)
                    apart(dve)
                    nc.vector.bn_aggr(x_mv[:, b], x_stats[:, b]).then_inc(x_mv_made, 1)

            def mask_of(f, k):
                wait(dve, ld_mask[k], 8 * (f - k) + 16)
                wait(dve, bias_b_made, CG * (f - 1))
                nc.vector.tensor_scalar(mask_add[:, k], mask_u8[:, k], MASKED, -MASKED, ALU.mult,
                                        ALU.add).then_inc(mask_made, 1)

            def front(f, slot, kind, i):
                use = USE[kind, i]
                ps = ps_proj[use % 2]
                if kind == "x":
                    wait(dve, xt_hi_made, KT * f + KX * (i + 1))
                    for j in range(KX):
                        k = KX * i + j
                        ins = nc.vector.scalar_tensor_tensor(
                            out=xt_lo[:, k], in0=ps[:, TOK * j:TOK * (j + 1)], scalar=gin_col[:, k:k + 1],
                            in1=xt_hi[:, k].bitcast(F32), op0=ALU.mult, op1=ALU.subtract)
                    ins.then_inc(proj_read, 1)
                elif kind == "v":
                    wait(dve, v_hi_made, 3 * (f + 1))
                    for from_, hi, to in copies_of_v(ps, v_hi, v_lo, vd_hi, vd_lo, slot):
                        ins = nc.vector.tensor_tensor(to, from_, hi.bitcast(F32), ALU.subtract)
                    ins.then_inc(proj_read, 1)
                else:
                    for half in range(2):
                        up, across = slice(DH * half, DH * (half + 1)), slice(DH * (1 - half), DH * (2 - half))
                        wait(dve, q_hi_made, 2 * QT * f + 2 * i + half + 1)
                        ins = nc.vector.tensor_tensor(q_place(across, slot, 2 * i + half),
                                                      ps[up, 0:TOK].rearrange("p (t n) -> p t n", n=HALF),
                                                      q_place(up, slot, 2 * i + half).bitcast(F32), ALU.subtract)
                    ins.then_inc(proj_read, 1)

            for z in (v_hi, v_lo):
                nc.vector.memset(z[:, :, :, 0:DH].bitcast(F32), 0.0)
                nc.vector.memset(z[:, :, :, 2 * DH:3 * DH].bitcast(F32), 0.0)
            for z in (vd_hi, vd_lo):
                nc.vector.memset(z[0:DH, :, :, DH:2 * DH].bitcast(F32), 0.0)
                nc.vector.memset(z[DH:P, :, :, 0:DH].bitcast(F32), 0.0)
            nc.vector.memset(v_raw[DH:P, 0:HALF], 0.0)
            nc.vector.memset(eps_col[:], EPS)
            nc.vector.memset(pow_col[:], -0.5)
            nc.vector.memset(minus_one[:], -1.0)
            nc.vector.memset(logit_bot[:, :, :, N:N + 1], 0.0)
            nc.vector.memset(logit_top[:, :, :, HALF:HALF + 1], 0.0).then_inc(filled, 1)
            x_stats_of(0)
            x_mean_var_of(0)
            dve.wait_ge(wkv_hi_made, 1)
            nc.vector.tensor_tensor(wkv_lo[:].rearrange("p k n -> p (k n)"), wkv_raw,
                                    wkv_hi[:].rearrange("p k n -> p (k n)").bitcast(F32),
                                    ALU.subtract).then_inc(wkv_lo_made, 1)
            dve.wait_ge(ld_cols, 16 * COL_LOADS)
            nc.vector.tensor_scalar(k_shift[:], nk_col[:], -SCALE, None, ALU.mult).then_inc(shifts_made, 1)
            nc.vector.tensor_scalar(v_shift[:], nv_col[:], -1.0, None, ALU.mult).then_inc(shifts_made, 1)
            mask_of(0, 0)

            def wq_low(i):
                dve.wait_ge(wq_hi_made, i + 1)
                nc.vector.tensor_tensor(wq_piece(wq_lo, i), raw_piece(i, KT), wq_piece(wq_hi, i).bitcast(F32),
                                        ALU.subtract).then_inc(wq_lo_made, 1)

            def wo_low(i):
                dve.wait_ge(wo_hi_made, i + 1)
                nc.vector.tensor_tensor(wo_piece(wo_lo, i), raw_piece(i, OT // WP), wo_piece(wo_hi, i).bitcast(F32),
                                        ALU.subtract).then_inc(wo_lo_by_dve, 1)

            def shift_bias():
                dve.wait_ge(ld_rows, 16 * ROW_LOADS)
                dve.wait_ge(ld_bias, 16 * BIAS_LOADS)
                for cols_, keys_ in ((slice(0, BOT), N), (slice(BOT, BOT + TOP), HALF)):
                    part = bias_c[:, :, cols_].rearrange("p c (e n) -> p c e n", e=2)
                    nc.vector.tensor_tensor(part, part, nb_row[:].unsqueeze(3).to_broadcast([P, CB, 2, keys_]),
                                            ALU.subtract).then_inc(bias_shifted, 1)

            between = {
                ("x", 1): lambda: (wq_low(0), shift_bias(), wq_low(1), x_stats_of(1), x_mean_var_of(1)),
                ("v", 0): lambda: wq_low(2),
            }
            first_extras = {
                0: lambda: wq_low(3),
                1: lambda: mask_of(1, 1),
                4: lambda: wo_low(2),
                5: lambda: wo_low(3),
            }
            for part in PROLOGUE:
                if part[0] != "kv":
                    front(0, 0, *part)
                if part in between:
                    between[part]()

            def read_front(p, t, first, last):
                for f, slot, kind, i in front_parts(p, t, first, last):
                    if kind != "kv":
                        front(f, slot, kind, i)

            def body(p, first, last):
                for t in steps(last):
                    n = CP * p + t
                    early = first and t < 3
                    if early:
                        read_front(p, t - 1, first, last)
                    if t < CP:
                        scores_low(n, t)
                    if live(t, LAG_SUM, first, last):
                        inverse(n - LAG_SUM, t - LAG_SUM)
                    if done := out_batch(p, t, STEP_OUT_STATS + 1, first, last):
                        out_mean_var(*done)
                    if not last and t % CG == STEP_STATS + 1:
                        x_mean_var_of(2 * p + t // CG + 2)
                    if t < CP:
                        logits(n, t)
                    if first and t in first_extras:
                        first_extras[t]()
                    if live(t, LAG_HEADS, first, last) and (t - LAG_HEADS) % 2:
                        heads_lo(pair(p, t - LAG_HEADS), t - LAG_HEADS)
                    if not early:
                        read_front(p, t - 1, first, last)
                    if live(t, LAG_T, first, last):
                        weights_lo(n - LAG_T, pair(p, t - LAG_T), t - LAG_T)
                    if done := out_batch(p, t, STEP_OUT_STATS, first, last):
                        out_stats(*done)
                    if not last:
                        if t % CG == STEP_STATS:
                            x_stats_of(2 * p + t // CG + 2)
                        if t % CG == STEP_MASK:
                            mask_of(2 * p + t // CG + 2, t // CG)

            run_pairs(dve, body)

        @block.scalar
        def _(act):
            def weights_hi(n, u, t):
                s = t % 4
                wait(act, wt_done, n + 1)
                wait(act, pv_done, u - 1)
                nc.scalar.copy(wt_hi[:, s], ps_wt[:]).then_inc(wt_hi_made, 1)

            def exponentials(n, t):
                s = t % 2
                wait(act, nrm_made, n - 1)
                wait(act, inv_made, n - 1)
                for j in range(HC):
                    if j % 2 == 0:
                        wait(act, s_read, 2 * n + j // 2 + 1)
                    out_, in_ = ((exp_bot, logit_bot), (exp_top, logit_top))[j // 2]
                    ins = nc.scalar.activation(out_[:, s, j % 2], in_[:, s, j % 2], ACT.Exp, bias=neg_max[:, s, j:j + 1],
                                               scale=-1.0, accum_out=w_sum[:, s, j:j + 1])
                ins.then_inc(exp_made, 1)

            def heads_hi(u, t):
                s = t // 2 % 2
                wait(act, pv_done, u + 1)
                wait(act, o_done, 2 * u - 2)
                nc.scalar.activation(o_hi[:, s], ps_pv[:], ACT.Identity, bias=nv_col[:, 0:1]).then_inc(o_hi_made, 1)

            def out_norm(batch, back):
                b = back % GB
                wait(act, y_shift_made, batch + 1)
                wait(act, y_out_made, batch - 1)
                nc.scalar.activation(y_nrm[:, b], ps_o[b][:], ACT.Identity, bias=y_shift[:, b:b + 1],
                                     scale=y_rstd[:, b:b + 1]).then_inc(y_nrm_made, 1)

            def x_norm(f):
                wait(act, x_shift_made, f + 1)
                wait(act, proj_done, USES * (f - 1) + XT)
                for b in range(GB):
                    nc.scalar.activation(xn[:, b], x_in[:, b], ACT.Identity, bias=x_shift[:, b:b + 1],
                                         scale=x_rstd[:, b:b + 1]).then_inc(xn_made, 1)

            def front(f, slot, kind, i):
                use = USE[kind, i]
                ps = ps_proj[use % 2]
                if kind == "x":
                    wait(act, proj_done, USES * f + use + 1)
                    for j in range(KX):
                        k = KX * i + j
                        nc.scalar.activation(xt_hi[:, k], ps[:, TOK * j:TOK * (j + 1)], ACT.Copy,
                                             scale=gin_col[:, k:k + 1]).then_inc(xt_hi_made, 1)
                elif kind == "kv":
                    wait(act, proj_done, USES * f + use + 1)
                    wait(act, k_lo_made, f)
                    for half in range(2):
                        nc.scalar.activation(k_raw[DH * half:DH * (half + 1)], ps[0:DH, 0:TOK], ACT.Identity,
                                             bias=k_shift[:, 0:1], scale=SCALE).then_inc(k_raw_made, 1)
                    nc.scalar.activation(v_raw[DH:P, HALF:], ps[DH:P, 0:TOK], ACT.Identity,
                                         bias=v_shift[DH:P, 0:1]).then_inc(v_raw_made, 1)
                    wait(act, k_raw_made, 2 * f + 2)
                    nc.scalar.copy(keys[:, slot, :, 0],
                                   k_raw[:].rearrange("p (b n) -> p b n", b=GB)).then_inc(k_hi_made, 1)
                elif kind == "v":
                    wait(act, proj_done, USES * f + use + 1)
                    for from_, hi, _ in copies_of_v(ps, v_hi, v_lo, vd_hi, vd_lo, slot):
                        nc.scalar.copy(hi, from_).then_inc(v_hi_made, 1)
                else:
                    wait(act, proj_done, USES * f + use + 1)
                    for half in range(2):
                        up = slice(DH * half, DH * (half + 1))
                        nc.scalar.copy(q_place(up, slot, 2 * i + half),
                                       ps[up, 0:TOK].rearrange("p (t n) -> p t n", n=HALF)).then_inc(q_hi_made, 1)

            act.wait_ge(ld_wkv, 16)
            nc.scalar.copy(wkv_hi[:].rearrange("p k n -> p (k n)"), wkv_raw).then_inc(wkv_hi_made, 1)
            x_norm(0)
            act.wait_ge(ld_cols, 16 * COL_LOADS)
            act.wait_ge(filled, 1)

            def wq_high(i):
                act.wait_ge(ld_wq[i], 16)
                nc.scalar.copy(wq_piece(wq_hi, i), raw_piece(i, KT)).then_inc(wq_hi_made, 1)

            def wo_high(i):
                act.wait_ge(ld_wo[i], 16)
                nc.scalar.copy(wo_piece(wo_hi, i), raw_piece(i, OT // WP)).then_inc(wo_hi_made, 1)

            between = {
                ("x", 1): lambda: (wq_high(0), wq_high(1), act.wait_ge(shifts_made, 2)),
                ("q", 0): lambda: wq_high(2),
                ("q", 1): lambda: wq_high(3),
                ("q", 3): lambda: x_norm(1),
            }
            first_extras = {
                1: lambda: (wo_high(0), wo_high(1)),
                3: lambda: wo_high(2),
                4: lambda: wo_high(3),
            }
            for part in PROLOGUE:
                front(0, 0, *part)
                if part in between:
                    between[part]()

            def body(p, first, last):
                for t in steps(last):
                    n = CP * p + t
                    if live(t, LAG_HEADS, first, last) and (t - LAG_HEADS) % 2:
                        heads_hi(pair(p, t - LAG_HEADS), t - LAG_HEADS)
                    for f, slot, kind, i in front_parts(p, t - 1, first, last):
                        front(f, slot, kind, i)
                    if live(t, LAG_T, first, last):
                        weights_hi(n - LAG_T, pair(p, t - LAG_T), t - LAG_T)
                    if done := out_batch(p, t, STEP_OUT_NORM, first, last):
                        out_norm(*done)
                    if first and t in first_extras:
                        first_extras[t]()
                    if t < CP:
                        exponentials(n, t)
                    if not last and t % CG == STEP_XN:
                        x_norm(2 * p + t // CG + 2)

            run_pairs(act, body)

        @block.gpsimd
        def _(pool):
            def masked_bias(n, g, t):
                slot, b, c, s = t // CG % 2, t // CB % GB, t % CB, t % 2
                if t % CG == 0:
                    wait(pool, mask_made, g + 1)
                wait(pool, s_low_made, 2 * (n - 1))
                for out_, bias in zip(bot_top(bias_b[:, s]), bot_top(bias_c[:, c])):
                    keys_ = out_.shape[2]
                    key_mask = mask_add[:, slot, b, 0:keys_].unsqueeze(1).to_broadcast([P, 2, keys_])
                    ins = nc.gpsimd.tensor_tensor(out_, bias, key_mask, ALU.add)
                ins.then_inc(bias_b_made, 1)

            def normalize(n, t):
                s = t % 2
                wait(pool, inv_made, n + 1)
                wait(pool, wt_done, n - 1)
                for i, (out_, w_exp) in enumerate(zip(bot_top(w_nrm[:, s]), (exp_bot, exp_top))):
                    keys_ = out_.shape[2]
                    ins = nc.gpsimd.tensor_tensor(out_, w_exp[:, s, :, 0:keys_],
                                                  w_inv[:, s, 2 * i:2 * i + 2].unsqueeze(2).to_broadcast([P, 2, keys_]),
                                                  ALU.mult)
                ins.then_inc(nrm_made, 1)

            def x_rstd_of(f):
                wait(pool, x_mv_made, GB * (f + 1))
                wait(pool, x_rstd_made, f)
                nc.gpsimd.tensor_tensor(x_var[:], x_mv[:, :, 1], eps_col[:], ALU.add).then_inc(x_var_made, 1)
                wait(pool, x_var_made, f + 1)
                wait(pool, xn_made, GB * f)
                nc.gpsimd.tensor_tensor(x_rstd[:], x_var[:], pow_col[:], ALU.pow).then_inc(x_rstd_made, 1)
                wait(pool, x_rstd_made, f + 1)
                wait(pool, x_shift_made, f)
                nc.gpsimd.tensor_tensor(x_mr[:], x_mv[:, :, 0], x_rstd[:], ALU.mult).then_inc(x_mr_made, 1)
                wait(pool, x_mr_made, f + 1)
                nc.gpsimd.tensor_tensor(x_shift[:], x_mr[:], minus_one[:], ALU.mult).then_inc(x_shift_made, 1)

            def y_scale(batch, back):
                b = back % GB
                c = slice(b, b + 1)
                wait(pool, y_mv_made, batch + 1)
                wait(pool, y_nrm_made, batch - 1)
                nc.gpsimd.tensor_tensor(y_var[:, c], y_mv[:, b, 1:2], eps_col[:, 0:1], ALU.add).then_inc(y_var_made, 1)
                wait(pool, y_var_made, batch + 1)
                nc.gpsimd.tensor_tensor(y_rstd[:, c], y_var[:, c], pow_col[:, 0:1], ALU.pow).then_inc(y_rstd_made, 1)
                wait(pool, y_rstd_made, batch + 1)
                apart(pool)
                nc.gpsimd.tensor_scalar(y_shift[:, c], y_mv[:, b, 0:1], -1.0, y_rstd[:, c], ALU.mult,
                                        ALU.mult).then_inc(y_shift_made, 1)

            def residual(batch, back):
                b = back % GB
                wait(pool, y_nrm_made, batch + 1)
                nc.gpsimd.tensor_tensor(y_nrm[:, b], y_nrm[:, b], gout_row[:], ALU.mult).then_inc(y_g_made, 1)
                wait(pool, y_g_made, batch + 1)
                wait(pool, ld_res[b], stored_before(batch, b) + 16)
                wait(pool, stored[b], stored_before(batch, b))
                nc.gpsimd.tensor_tensor(y_out[:, b], y_nrm[:, b], x_res[:, b], ALU.add).then_inc(y_out_made, 1)

            def stored_before(batch, b):
                return 8 * (batch - b)

            def keys_lo(f, slot):
                wait(pool, k_hi_made, f + 1)
                nc.gpsimd.tensor_tensor(keys[:, slot, :, 1], k_raw[:].rearrange("p (b n) -> p b n", b=GB),
                                        keys[:, slot, :, 0].bitcast(F32), ALU.subtract).then_inc(k_lo_made, 1)

            nc.gpsimd.memset(ident[:], 0.0).then_inc(ident_zero, 1)
            pool.wait_ge(ident_zero, 1)
            nc.gpsimd.affine_select(out=ident[:], in_=ident[:], compare_op=ALU.not_equal, fill=1.0, base=0,
                                    pattern=[[-1, P]], channel_multiplier=1).then_inc(ident_made, 1)
            pool.wait_ge(filled, 1)
            x_rstd_of(0)

            def causal_bias(c):
                for u in range(2):
                    for i, part in enumerate(bot_top(bias_c[HALF * u:HALF * (u + 1), c])):
                        own = part[:, :, part.shape[2] - HALF:]
                        wait(pool, bias_made, 4 * c + 2 * u + i)
                        nc.gpsimd.affine_select(out=own, in_=own, compare_op=ALU.is_ge, fill=-MASKED, base=0,
                                                pattern=[[0, 2], [-1, HALF]], channel_multiplier=1).then_inc(bias_made, 1)
                pool.wait_ge(bias_made, 4 * (c + 1))

            pool.wait_ge(bias_shifted, 2)
            causal_bias(0)
            masked_bias(0, 0, 0)
            keys_lo(0, 0)
            x_rstd_of(1)
            for c in range(1, CB):
                causal_bias(c)

            def wo_low(i):
                pool.wait_ge(wo_hi_made, i + 1)
                nc.gpsimd.tensor_tensor(wo_piece(wo_lo, i), raw_piece(i, OT // WP), wo_piece(wo_hi, i).bitcast(F32),
                                        ALU.subtract).then_inc(wo_lo_by_pool, 1)

            first_extras = {
                1: lambda: wo_low(0),
                3: lambda: wo_low(1),
            }

            def body(p, first, last):
                for t in steps(last):
                    n = CP * p + t
                    if live(t, LAG_SUM, first, last):
                        normalize(n - LAG_SUM, t - LAG_SUM)
                    if t < CP and not (last and t == CP - 1):
                        masked_bias(n + 1, 2 * p + (t + 1) // CG, (t + 1) % CP)
                    if t < CP and t % CG == STEP_K_LO and not (last and t >= CG):
                        keys_lo(2 * p + t // CG + 1, (t // CG + 1) % 2)
                    if not last and t % CG == STEP_STATS + 1:
                        x_rstd_of(2 * p + t // CG + 2)
                    if done := out_batch(p, t, STEP_OUT_STATS + 1, first, last):
                        y_scale(*done)
                    if done := out_batch(p, t, STEP_OUT_ADD, first, last):
                        residual(*done)
                    if first and t in first_extras:
                        first_extras[t]()

            run_pairs(pool, body)


_INS = ["x", "fside_16xSxS_0", "cond_64", "mask_BxS_bk0", "L0_cond_g_in", "L0_cond_null_attn_bias", "L0_cond_Wq",
        "L0_cond_Wkv", "L0_cond_Wo", "L0_cond_g_out"]


def kernel(**inputs):
    import numpy as _np
    import concourse.bacc as _bacc
    from concourse import mybir as _mybir
    from concourse.bass_utils import run_bass_kernel_spmd as _run

    nc = _bacc.Bacc("TRN2", target_bir_lowering=False, num_devices=1)
    arrays, args = {}, []
    for name in _INS:
        a = _np.ascontiguousarray(inputs[name])
        arrays[f"in_{name}_dram"] = a
        args.append(nc.dram_tensor(f"in_{name}_dram", a.shape, _mybir.dt.from_np(a.dtype), kind="ExternalInput").ap())
    out = nc.dram_tensor("out_dram", (B, N, DIM), F32, kind="ExternalOutput").ap()
    attention_block(nc, *args, out)
    r = _run(nc, [arrays], core_ids=[0])
    return r.results[0]["out_dram"]
```
